# Optimizing a Trainium2 kernel written in Bass

```python
import numpy as np
import jax
import jax.numpy as jnp

def _softmax(x, axis=-1):
    return jax.nn.softmax(x, axis=axis)

def _gelu(x):
    return jax.nn.gelu(x, approximate=True)

def _silu(x):
    return jax.nn.silu(x)

def _sigmoid(x):
    return jax.nn.sigmoid(x)

def _layernorm(x, axis=-1, eps=1e-05):
    m = jnp.mean(x, axis=axis, keepdims=True)
    v = jnp.var(x, axis=axis, keepdims=True)
    return (x - m) / jnp.sqrt(v + eps)

def _scatter_add(tgt, idx, src, axis=0):
    return tgt.at[idx].add(src)

def _segment_sum(src, seg, n):
    return jax.ops.segment_sum(src, seg, n)
kernel_name = 'mk_cond_resid_d2_seqx_r4_b8523d'

def setup_inputs(seed: int=0):
    np.random.seed(seed)
    _w = jnp.asarray

    def _rec_inputs():
        import jax
        import jax.numpy as jnp
        _rk = jax.random.key(seed)
        x = 7.22e-05 + 1 * jax.random.normal(jax.random.fold_in(_rk, 1), (8, 256, 256), jnp.float32)
        _lenS = 256 - jax.random.randint(jax.random.fold_in(_rk, 7), (8,), 0, max(1, 256 // 4) + 1, jnp.int32)
        _lenS2 = 256 - jax.random.randint(jax.random.fold_in(_rk, 8), (8,), 0, max(1, 256 // 4) + 1, jnp.int32)
        cond_2048 = 0.997298 + 0.498944 * jax.random.normal(jax.random.fold_in(_rk, 11), (8, 512), jnp.float32)
        return (x, cond_2048)
    x, cond_2048 = _rec_inputs()

    def _L0_cond_setup():
        import jax, jax.numpy as jnp
        import numpy as np
        EPS_IN = 1e-05
        EPS_DM = 1e-08

        def _dcoef(weight, style):
            return jax.lax.rsqrt(jnp.einsum('oi,bi->bo', jnp.square(weight), jnp.square(style)) + EPS_DM)
        key = jax.random.key(seed)
        ks = jax.random.split(key, 7)
        B, S, H = (8, 256, 256)
        lim = 1.0 / np.sqrt(H)
        u = lambda k, shp: jax.random.uniform(k, shp, jnp.float32, -lim, lim)
        return {'x': jax.random.normal(ks[0], (B, S, H), jnp.float32), 'q_weight': u(ks[1], (H, H)), 'k_weight': u(ks[2], (H, H)), 'v_weight': u(ks[3], (H, H)), 'w_weight': u(ks[4], (H, H)), 'u_weight': u(ks[5], (H, H)), 'styles': jax.random.normal(ks[6], (B, 2 * H), jnp.float32) * 0.5 + 1.0, 'num_heads': 16}
    _L0_cond_all = _L0_cond_setup()
    _L0_cond_in = {k: v for k, v in _L0_cond_all.items() if k in ('q_weight', 'k_weight', 'v_weight', 'w_weight', 'u_weight')}
    del _L0_cond_all

    def _L1_cond_setup():
        import jax, jax.numpy as jnp
        import numpy as np
        B, S, D_MODEL, D_INNER, D_STATE = (4, 1024, 256, 512, 16)
        key = jax.random.key(seed)
        ks = jax.random.split(key, 12)
        inp = {'x': jax.random.normal(ks[0], (B, S, D_MODEL), jnp.float32), 't_emb': jax.random.normal(ks[1], (B, D_INNER), jnp.float32), 'W_in': jax.random.normal(ks[2], (2 * D_INNER, D_MODEL), jnp.float32) * 0.02, 'W_conv': jax.random.normal(ks[3], (D_INNER, 1, 4), jnp.float32) * 0.1, 'b_conv': jnp.zeros((D_INNER,), jnp.float32), 'ln_g': jnp.ones((D_INNER,), jnp.float32), 'ln_b': jnp.zeros((D_INNER,), jnp.float32), 'W_xproj': jax.random.normal(ks[4], (3 * D_STATE, D_INNER), jnp.float32) * 0.02, 'W_dt': jax.random.normal(ks[5], (D_STATE, D_STATE), jnp.float32) * 0.01, 'b_dt': jax.random.uniform(ks[6], (D_STATE,), jnp.float32) * 0.1, 'A_log': jax.random.normal(ks[7], (D_STATE,), jnp.float32) * 0.1, 'D': jnp.ones((D_INNER,), jnp.float32) * 0.1, 'W_out': jax.random.normal(ks[8], (D_MODEL, D_INNER), jnp.float32) * 0.02}
        return inp
    _L1_cond_all = _L1_cond_setup()
    _L1_cond_in = {k: v for k, v in _L1_cond_all.items() if k in ('W_in', 'W_conv', 'b_conv', 'ln_g', 'ln_b', 'W_xproj', 'W_dt', 'b_dt', 'A_log', 'D', 'W_out')}
    del _L1_cond_all
    return {'x': x, 'cond_2048': cond_2048, 'L0_cond_q_weight': _L0_cond_in['q_weight'], 'L0_cond_k_weight': _L0_cond_in['k_weight'], 'L0_cond_v_weight': _L0_cond_in['v_weight'], 'L0_cond_w_weight': _L0_cond_in['w_weight'], 'L0_cond_u_weight': _L0_cond_in['u_weight'], 'L1_cond_W_in': _L1_cond_in['W_in'], 'L1_cond_W_conv': _L1_cond_in['W_conv'], 'L1_cond_b_conv': _L1_cond_in['b_conv'], 'L1_cond_ln_g': _L1_cond_in['ln_g'], 'L1_cond_ln_b': _L1_cond_in['ln_b'], 'L1_cond_W_xproj': _L1_cond_in['W_xproj'], 'L1_cond_W_dt': _L1_cond_in['W_dt'], 'L1_cond_b_dt': _L1_cond_in['b_dt'], 'L1_cond_A_log': _L1_cond_in['A_log'], 'L1_cond_D': _L1_cond_in['D'], 'L1_cond_W_out': _L1_cond_in['W_out']}

def reference(x, cond_2048, L0_cond_q_weight, L0_cond_k_weight, L0_cond_v_weight, L0_cond_w_weight, L0_cond_u_weight, L1_cond_W_in, L1_cond_W_conv, L1_cond_b_conv, L1_cond_ln_g, L1_cond_ln_b, L1_cond_W_xproj, L1_cond_W_dt, L1_cond_b_dt, L1_cond_A_log, L1_cond_D, L1_cond_W_out):
    import jax
    import jax.numpy as jnp

    def _L0_cond_ref(x, q_weight, k_weight, v_weight, w_weight, u_weight, styles, num_heads):
        import jax, jax.numpy as jnp
        import numpy as np
        EPS_IN = 1e-05
        EPS_DM = 1e-08

        def _dcoef(weight, style):
            return jax.lax.rsqrt(jnp.einsum('oi,bi->bo', jnp.square(weight), jnp.square(style)) + EPS_DM)
        B, S, H = x.shape
        nh = num_heads
        d = H // nh
        scale = jnp.asarray(d, x.dtype) ** (-0.5)
        s1 = styles[:, :H]
        s2 = styles[:, H:]
        x = x * s1[:, None, :]
        mu = jnp.mean(x, axis=-1, keepdims=True)
        var = jnp.mean(jnp.square(x - mu), axis=-1, keepdims=True)
        x = (x - mu) * jax.lax.rsqrt(var + EPS_IN)
        q_dc = _dcoef(q_weight, s1)
        k_dc = _dcoef(k_weight, s1)
        v_dc = _dcoef(v_weight, s1)
        w_dc = _dcoef(w_weight, s2)
        u_dc = _dcoef(u_weight, s2)

        def heads(t):
            return t.reshape(B, S, nh, d).transpose(0, 2, 1, 3)
        q = heads(jnp.einsum('bsh,oh->bso', x, q_weight) * q_dc[:, None, :])
        k = heads(jnp.einsum('bsh,oh->bso', x, k_weight) * k_dc[:, None, :])
        v_flat = jnp.einsum('bsh,oh->bso', x, v_weight) * v_dc[:, None, :] * s2[:, None, :]
        skip = v_flat
        v = heads(v_flat)
        attn = jnp.einsum('bhqd,bhkd->bhqk', q, k) * scale
        attn = jax.nn.softmax(attn, axis=-1)
        out = jnp.einsum('bhqk,bhkd->bhqd', attn, v).transpose(0, 2, 1, 3).reshape(B, S, H)
        out = jnp.einsum('bsh,oh->bso', out, w_weight) * w_dc[:, None, :]
        skip = jnp.einsum('bsh,oh->bso', skip, u_weight) * u_dc[:, None, :]
        return out + skip

    def _L1_cond_ref(x, t_emb, W_in, W_conv, b_conv, ln_g, ln_b, W_xproj, W_dt, b_dt, A_log, D, W_out):
        import jax, jax.numpy as jnp
        import numpy as np
        B, S, D_MODEL, D_INNER, D_STATE = (4, 1024, 256, 512, 16)
        d_inner = W_conv.shape[0]
        d_state = A_log.shape[0]
        xr, gate = jnp.split(x @ W_in.T, 2, axis=-1)
        xr = xr + t_emb[:, None, :]
        xc = jax.lax.conv_general_dilated(xr.transpose(0, 2, 1), W_conv, (1,), [(3, 0)], feature_group_count=d_inner, dimension_numbers=('NCH', 'OIH', 'NCH')) + b_conv[None, :, None]
        xc = jax.nn.silu(xc).transpose(0, 2, 1)
        mu = xc.mean(-1, keepdims=True)
        var = xc.var(-1, keepdims=True)
        xn = (xc - mu) / jnp.sqrt(var + 1e-05) * ln_g + ln_b
        Bm, Cm, dt = jnp.split(xn @ W_xproj.T, 3, axis=-1)
        dt = jnp.tanh(dt @ W_dt.T + b_dt) * 0.01
        A = -jnp.tanh(A_log)
        Ad = 1.0 + dt * A
        Bd = Bm * jnp.minimum(jnp.linalg.norm(xn, axis=-1, keepdims=True), 1.0)
        h0 = jnp.zeros((xn.shape[0], d_state, d_inner), xn.dtype)

        def step(h, inputs):
            ad, bd, xt, ct = inputs
            h = jnp.clip(h * ad[:, :, None] + bd[:, :, None] * xt[:, None, :], -10.0, 10.0)
            yt = jnp.einsum('bd,bdh->bh', ct, h)
            return (h, yt)
        _, ys = jax.lax.scan(step, h0, (Ad.transpose(1, 0, 2), Bd.transpose(1, 0, 2), xn.transpose(1, 0, 2), Cm.transpose(1, 0, 2)))
        y = ys.transpose(1, 0, 2) + D * xn
        return y * jax.nn.silu(gate) @ W_out.T
    x = x + _L0_cond_ref(x, L0_cond_q_weight, L0_cond_k_weight, L0_cond_v_weight, L0_cond_w_weight, L0_cond_u_weight, cond_2048, 16)
    x = x + _L1_cond_ref(x, cond_2048, L1_cond_W_in, L1_cond_W_conv, L1_cond_b_conv, L1_cond_ln_g, L1_cond_ln_b, L1_cond_W_xproj, L1_cond_W_dt, L1_cond_b_dt, L1_cond_A_log, L1_cond_D, L1_cond_W_out)
    return x

_drawn_inputs = setup_inputs


def setup_inputs(seed=0):
    import zlib

    import numpy as np

    out = dict(_drawn_inputs(seed))
    spreads = {'L1_cond_b_conv': (0.0, 0.1),
     'L1_cond_ln_g': (1.0, 0.2),
     'L1_cond_ln_b': (0.0, 0.1),
     'L1_cond_D': (0.10000000149011612, 0.6)}
    factors = {'L1_cond_W_dt': 27.276, 'L1_cond_b_dt': 23.088, 'L1_cond_A_log': 8.0}
    for name, (base, spread) in spreads.items():
        noise = np.random.default_rng([zlib.crc32(name.encode()), seed]).standard_normal(out[name].shape)
        drawn = base * np.exp(spread * noise) if base else spread * noise
        out[name] = jnp.asarray(drawn.astype(out[name].dtype))
    for name, factor in factors.items():
        out[name] = (out[name] * factor).astype(out[name].dtype)
    return out
```

```python
from contextlib import ExitStack

import numpy as np

import concourse.bass as bass
from concourse import mybir

F32 = mybir.dt.float32
BF16 = mybir.dt.bfloat16
ALU = mybir.AluOpType
ACT = mybir.ActivationFunctionType
AX = mybir.AxisListType

P = 128
B, S, H = 8, 256, 256
NH, HD = 16, 16
C, NS = 512, 16
TAPS = 4
HALVES = S // P
NT = B * HALVES
HT, CT = H // P, C // P
BOUND = 10.0
STEP = 0.01
SCALE = float(HD) ** -0.5
EPS_LN, EPS_DM = 1e-5, 1e-8
NP3 = 3 * NS
PAIRS = [(0, 0), (1, 0), (2, 0), (0, 1), (1, 1), (0, 2)]
KX = len(PAIRS) * B
KU = KX + 3
CH = 8
NCH = S // CH
BD_J = B * (S * P)


class Own:

    def __init__(self, eng, sem):
        self.eng, self.sem, self.base, self.n, self.start = eng, sem, 0, 0, 0

    def enter(self, i, per):
        self.start += self.n
        self.n, self.per = 0, per
        self.base = i * per + self.start

    def leave(self, trips):
        assert self.n == self.per, (self.n, self.per)
        self.start += trips * self.per
        self.base, self.n = self.start, 0

    def mark(self, ins):
        ins.then_inc(self.sem, 1)
        self.n += 1

    def settle(self, back=0):
        self.eng.wait_ge(self.sem, self.base + self.n - back)


def build(nc, x_tok, xT, s1_row, condT, w5T, winT, wconv, bconv, ln_row, lnT, wxT, wxdt, wdtT, bdt_row, alog_row,
          woT, ident_d, mask8_d, sel_d, parity_d, out):
    with ExitStack() as ctx:
        def sb(name, shape, dt=F32):
            return ctx.enter_context(nc.sbuf_tensor(name, shape, dt))

        def sem(name):
            return ctx.enter_context(nc.semaphore(name))

        xs_d = nc.dram_tensor("xs_d", (3, B, S, C), BF16, kind="Internal").ap()
        bd_d = nc.dram_tensor("bd_d", (KU * S * P + 2 * B * NS,), BF16, kind="Internal").ap()
        y_d = nc.dram_tensor("y_d", (S, B, C), F32, kind="Internal").ap()

        bank = [ctx.enter_context(nc.psum_tensor(f"bank{i}", [P, 512], F32)) for i in range(8)]

        ident = sb("ident", [P, P])
        mask8 = sb("mask8", [P, B])
        sel = sb("sel", [P, 4, P], BF16)
        parity = sb("parity", [P, 2])
        ones = sb("ones", [P, P])
        cond = sb("cond", [P, CT, B])
        w5 = sb("w5", [P, 5, HT, H])
        win = sb("win", [P, HT, 2 * C])
        wcv = sb("wcv", [P, CT, TAPS])
        bcv = sb("bcv", [P, CT])
        lnt = sb("lnt", [P, 2, CT])
        lnr = sb("lnr", [P, 3, C])
        wx = sb("wx", [P, CT, NP3])
        wxg = sb("wxg", [P, CT, NP3])
        wxd = sb("wxd", [NS, C])
        wdt = sb("wdt", [NS, NS])
        bdt = sb("bdt", [P, NS])
        tA = sb("tA", [P, NS])
        wo = sb("wo", [P, CT, H])
        lnb_rep = sb("lnb_rep", [P, CT, P])
        proj_sum = sb("proj_sum", [P, NP3])
        proj_off = sb("proj_off", [P, NP3])
        cond2 = sb("cond2", [P, CT, B])
        dc = sb("dc", [P, 5, HT, B])
        dcv = sb("dcv", [P, 5, HT, B])
        dct = sb("dct", [P, 5, HT, B])
        kdc = sb("kdc", [P, B, HT, 2])
        vdc = sb("vdc", [P, HT, B])
        half_ones = sb("half_ones", [P, 2, 2 * HD])

        xres = sb("xres", [P, HT, B * S])
        raw = sb("raw", [P, NT, NP3])
        mv = sb("mv", [P, NT, 2])
        bn = sb("bn", [P, NT, 6])
        tick = sb("tick", [P, 1])
        var_e = sb("var_e", [P, NT])
        rt = sb("rt", [P, NT])
        rs = sb("rs", [P, NT])
        ybias = sb("ybias", [P, NT])

        hi = sb("hi", [P, S])
        cP = sb("cP", [P, S])
        ZR = 8
        zst = sb("zst", [P, ZR, C])
        cst = sb("cst", [P, 2, CH, 32])
        xst = sb("xst", [64, 2, CH, C], BF16)
        bst = sb("bst", [64, 2, CH, P], BF16)
        yb = sb("yb", [P, 2, CH // 4, C])
        l0 = ExitStack()

        def sb0(name, shape, dt=F32):
            return l0.enter_context(nc.sbuf_tensor(name, shape, dt))

        xt = sb0("xt", [P, NT, H])
        s1b = sb0("s1b", [P, B, H])
        wsq = sb0("wsq", [P, 5, HT, H])
        xnb = sb0("xnb", [P, HALVES, H])
        xnT = sb0("xnT", [P, HT, S])
        qT = sb0("qT", [P, HT, S])
        kT = sb0("kT", [P, 2, HT, S])
        vT = sb0("vT", [P, HT, S])
        vp = sb0("vp", [P, HALVES, NH // 2, 4, HD])
        mx = sb0("mx", [P, HALVES, P])
        mT = sb0("mT", [P, S], BF16)
        ex = sb0("ex", [P, 2, 4, 512])
        sel32 = sb0("sel32", [P, 4, P])
        rec = sb0("rec", [P, HT, S])
        attT = sb0("attT", [P, HT, S])
        l0.close()
        gateT = sb("gateT", [P, CT, B * S])
        xc = sb("xc", [P, NT, C])
        l1 = ExitStack()

        def sb1(name, shape, dt=F32):
            return l1.enter_context(nc.sbuf_tensor(name, shape, dt))

        ss = sb1("ss", [P, NT])
        nrm = sb1("nrm", [P, NT])
        t48 = sb1("t48", [P, NT, NP3])
        adt = sb1("adt", [P, HALVES, B, NS])
        cdt = sb1("cdt", [P, HALVES, B, NS])
        bnt = sb1("bnt", [P, HALVES, B, NS])
        dtt = sb1("dtt", [P, NT, NS])
        pcum = sb1("pcum", [P, S])
        one_row = sb1("one_row", [P, S])
        ipc = sb1("ipc", [P, S])
        rr = sb1("rr", [P, S + 1])
        dr = sb1("dr", [P, S])
        bpart = sb1("bpart", [P, 3, HALVES, B * NS], BF16)
        dpart = sb1("dpart", [P, 3, HALVES, B * NS], BF16)
        brem = sb1("brem", [P, HALVES, B * NS])
        drem = sb1("drem", [P, HALVES, B * NS])
        zeros = sb1("zeros", [P, 2048], BF16)
        conv_bufs = ExitStack()

        def sbc(name, shape, dt=F32):
            return conv_bufs.enter_context(nc.sbuf_tensor(name, shape, dt))

        xrp = sbc("xrp", [P, CT, TAPS - 1 + S])
        acc = sbc("acc", [P, CT, S])
        xcT = sbc("xcT", [P, CT, S])
        conv_bufs.close()
        xpart = sb1("xpart", [P, 2, 3, C], BF16)
        xrem = sb1("xrem", [P, 2, C])
        xn = sb1("xn", [P, 2, C])
        sqj = sb1("sqj", [P, C])
        l1.close()
        ytk = sb("ytk", [P, 2, C])
        ysum = sb("ysum", [P, 2, C])
        yg = sb("yg", [P, CT, P])
        x1s = sb("x1s", [P, HT, S])
        ob = sb("ob", [P, 2, H])

        names = """ld_l0 ld_w ld_mod ld_x ld_l1 ld_c zfill vec act_own pool_own const_pool dcsum dc_done rt_in rt_out
            xnb_ready tr_done xnT_ready qkv_done qkv_ready smax_done maxes mt_done mT_ready st_done exp_done pv_done
            att_ready wu_done x1_ready wcomp wgain pconst xr_done xr_in tap3_ready gate_done gate_out conv_done
            conv_used xcT_ready xcT_used bcd_done raw_ready tok_ready tok_taken stats_ready xn_ready sq_done part0 part1
            rem0 rem1 parts_ready parts_out xs_out dx_ready ss_ready nrm_ready dt_in dt_out eb_ready eb_tr ipc_ready
            eb_back bsplit bd_out c_ready ld_x0 ld_b0 ld_x1 ld_b1 u_done z_ready y_done y_taken yst0 yst1 cst_ready ld_y0 ld_y1
            ysum_ready yt_done yg_ready o_done ob_ready o_out x1s_ready xone_ready""".split()
        s = {n: sem(n) for n in names}

        block = ctx.enter_context(nc.Block())

        @block.sync
        def _(sp):
            for dst, src in ((xt[:, :, :], x_tok), (s1b[:, :, :], s1_row.partition_broadcast(P))):
                sp.dma_start(dst, src).then_inc(s["ld_l0"], 16)
            for dst, src in ((w5[:, :, :, :], w5T), (cond[:, :, :], condT)):
                sp.dma_start(dst, src).then_inc(s["ld_w"], 16)
            for dst, src in ((ident[:, :], ident_d), (sel32[:, :, :], sel_d), (parity[:, :], parity_d),
                             (mask8[:, :], mask8_d)):
                sp.dma_start(dst, src).then_inc(s["ld_c"], 16)
            sp.dma_start(xres[:, :, :], xT).then_inc(s["ld_x"], 16)
            for dst, src in ((win[:, :, :], winT), (wcv[:, :, :], wconv), (bcv[:, :], bconv), (lnt[:, :, :], lnT),
                             (lnr[:, :, :], ln_row.partition_broadcast(P)), (wx[:, :, :], wxT), (wxd[:, :], wxdt),
                             (wdt[:, :], wdtT), (bdt[:, :], bdt_row.partition_broadcast(P)),
                             (tA[:, :], alog_row.partition_broadcast(P)), (wo[:, :, :], woT)):
                sp.dma_start(dst, src).then_inc(s["ld_l1"], 16)
            with sp.Fori(0, B) as b:
                for t in range(HALVES):
                    sp.wait_ge(s["parts_ready"], b * HALVES + (t + 1))
                    sp.dma_start(xs_d[:, b, t * P:(t + 1) * P, :].rearrange("k p c -> p k c"), xpart[:, t, :, :])\
                      .then_inc(s["xs_out"], 16)
            sp.wait_ge(s["bsplit"], 2)
            sp.wait_ge(s["zfill"], 16)
            for j, (_, bp) in enumerate(PAIRS):
                rows = bd_d[j * BD_J:j * BD_J + B * (S * P + NS)].rearrange("(b q) -> b q", b=B)[:, 0:S * P]
                rows = rows.rearrange("b (t c) -> t b c", c=P)[:, :, 0:NS]
                for t in range(HALVES):
                    sp.dma_start(rows[t * P:(t + 1) * P], bpart[:, bp, t, :].rearrange("p (b d) -> p b d", b=B))\
                      .then_inc(s["bd_out"], 16)
            for k in range(3):
                row = bd_d[(KX + k) * S * P:(KX + k + 1) * S * P].rearrange("(t c) -> t c", c=P)
                for t in range(HALVES):
                    sp.dma_start(row[t * P:(t + 1) * P], dpart[:, k, t, :]).then_inc(s["bd_out"], 16)
            n_bd = (len(PAIRS) + 3) * HALVES
            sp.wait_ge(s["xs_out"], 16 * NT)
            sp.wait_ge(s["bd_out"], 16 * n_bd)
            bd_v = bd_d[0:KU * S * P].rearrange("(k t c) -> k t c", t=S, c=P)

            def load_chunk(par, ch):
                t0 = ch * CH
                at = 0
                for run in (3, 2, 1):
                    for k in range(run):
                        sp.dma_start(xst[at:at + B, par, :, :], xs_d[k, :, bass.ds(t0, CH), :])\
                          .then_inc(s[f"ld_x{par}"], 16)
                        at += B
                sp.dma_start(bst[0:KU, par, :, :], bd_v[:, bass.ds(t0, CH), :]).then_inc(s[f"ld_b{par}"], 16)

            def store_chunk(par, ch):
                for k in range(4):
                    sp.dma_start(y_d[bass.ds(ch * CH, CH), :, :].rearrange("(g k) b c -> k b g c", k=4)[k],
                                 yb[32 * k:32 * k + B, par, :, :]).then_inc(s[f"yst{par}"], 16)

            sp.wait_ge(s["xone_ready"], 1)
            load_chunk(0, 0)
            load_chunk(1, 1)
            with sp.Fori(0, NCH // 2 - 1) as i:
                for par in range(2):
                    sp.wait_ge(s["u_done"], i * (2 * CH) + (par + 1) * CH)
                    load_chunk(par, i * 2 + (par + 2))
                for par in range(2):
                    sp.wait_ge(s["y_taken"], i * (2 * CH // 4) + (par + 1) * (CH // 4))
                    store_chunk(par, i * 2 + par)
            for par in range(2):
                sp.wait_ge(s["y_taken"], (NCH // 2 - 1) * (2 * CH // 4) + (par + 1) * (CH // 4))
                store_chunk(par, NCH - 2 + par)
            sp.wait_ge(s["yst0"], NCH // 2 * 64)
            sp.wait_ge(s["yst1"], NCH // 2 * 64)
            for t in range(HALVES):
                sp.dma_start(ytk[:, t, :], y_d[t * P:(t + 1) * P, 0, :]).then_inc(s[f"ld_y{t}"], 16)
            with sp.Fori(0, B - 1) as b:
                for t in range(HALVES):
                    sp.wait_ge(s["ysum_ready"], b * HALVES + (t + 1))
                    sp.dma_start(ytk[:, t, :], y_d[t * P:(t + 1) * P, b + 1, :]).then_inc(s[f"ld_y{t}"], 16)

        @block.gpsimd
        def _(pool):
            own = Own(pool, s["pool_own"])
            nc.gpsimd.memset(vp[:, :, :, :, :], 0.0)
            nc.gpsimd.memset(mx[:, :, :], 0.0)
            nc.gpsimd.memset(half_ones[:, :, :], 0.0)
            nc.gpsimd.memset(ones[:, :], 1.0)
            own.mark(nc.gpsimd.memset(cst[:, :, :, :], 0.0))
            own.settle()
            pool.wait_ge(s["ld_c"], 16 * 4)
            nc.gpsimd.tensor_copy(sel[:, :, :], sel32[:, :, :])
            nc.gpsimd.memset(half_ones[:, 0, 0:HD], 1.0)
            nc.gpsimd.memset(half_ones[:, 1, HD:2 * HD], 1.0).then_inc(s["const_pool"], 1)
            pool.wait_ge(s["x1_ready"], B)
            nc.gpsimd.memset(xrp[:, :, 0:TAPS - 1], 0.0)
            nc.gpsimd.memset(one_row[:, :], 1.0)
            nc.gpsimd.memset(rr[:, 0:1], BOUND)
            nc.gpsimd.memset(zst[:, ZR - 1, :], BOUND)
            own.mark(nc.gpsimd.memset(zeros[:, :], 0.0))
            own.settle()
            nc.gpsimd.memset(sqj[0:1, 0:1], 0.0).then_inc(s["const_pool"], 1)
            pool.dma_start(bd_d[0:KX * S * P].rearrange("(p r z) -> p r z", p=P, z=2048),
                           zeros[:, :].unsqueeze(1).broadcast_to([P, KX * S * P // (P * 2048), 2048]))\
                .then_inc(s["zfill"], 16)
            with pool.Fori(0, B) as b:
                for t in range(HALVES):
                    pool.wait_ge(s["xn_ready"], b * HALVES + (t + 1))
                    nc.gpsimd.tensor_tensor(xc[:, b * HALVES + t, :], xn[:, t, :], lnr[:, 2, :], ALU.mult)\
                        .then_inc(s["dx_ready"], 1)
            pool.wait_ge(s["c_ready"], 1)
            def fill_chunk(par, ch):
                nc.gpsimd.tensor_tensor(cst[:, par, :, 0:B],
                                        cP[:, bass.ds(ch * CH, CH)].unsqueeze(2).broadcast_to([P, CH, B]),
                                        mask8[:, :].unsqueeze(1).broadcast_to([P, CH, B]), ALU.mult)\
                    .then_inc(s["cst_ready"], 1)

            fill_chunk(0, 0)
            fill_chunk(1, 1)
            with pool.Fori(0, NCH // 2 - 1) as i:
                for par in range(2):
                    pool.wait_ge(s["y_done"], i * (2 * CH // 4) + (par + 1) * (CH // 4))
                    fill_chunk(par, i * 2 + (par + 2))
            with pool.Fori(0, B) as b:
                pool.wait_ge(s["o_done"], b * HALVES)
                nc.gpsimd.tensor_copy(x1s[:, :, :], xres[:, :, bass.ds(b * S, S)]).then_inc(s["x1s_ready"], 1)

        @block.scalar
        def _(act):
            act.wait_ge(s["rt_in"], 1)
            nc.scalar.activation(dct[:, :, :, :], dcv[:, :, :, :], ACT.Sqrt).then_inc(s["rt_out"], 1)
            act.wait_ge(s["rt_in"], 2)
            nc.scalar.activation(rt[:, :], var_e[:, :], ACT.Sqrt).then_inc(s["rt_out"], 1)
            act.wait_ge(s["dc_done"], 1)
            act.wait_ge(s["const_pool"], 1)
            with act.Fori(0, B) as b:
                act.wait_ge(s["tr_done"], b + 1)
                act.wait_ge(s["qkv_done"], b * 4)
                nc.scalar.activation(xnT[:, :, :], bank[0][:, :].rearrange("p (k s) -> p k s", k=HT), ACT.Copy)\
                    .then_inc(s["xnT_ready"], 1)
                act.wait_ge(s["qkv_done"], b * 4 + 1)
                act.wait_ge(s["st_done"], b * NH)
                for o in range(HT):
                    ins = nc.scalar.activation(qT[:, o, :], bank[2][:, o * S:(o + 1) * S], ACT.Copy,
                                               scale=dc[:, 0, o, bass.ds(b, 1)])
                ins.then_inc(s["qkv_ready"], 1)
                act.wait_ge(s["qkv_done"], b * 4 + 2)
                for o in range(HT):
                    for par in range(2):
                        ins = nc.scalar.activation(kT[:, par, o, :], bank[3][:, o * S:(o + 1) * S], ACT.Copy,
                                                   scale=kdc[:, b, o, par:par + 1])
                ins.then_inc(s["qkv_ready"], 1)
                act.wait_ge(s["qkv_done"], b * 4 + 3)
                act.wait_ge(s["wu_done"], b)
                for o in range(HT):
                    ins = nc.scalar.activation(vT[:, o, :], bank[4][:, o * S:(o + 1) * S], ACT.Copy,
                                               scale=vdc[:, o, bass.ds(b, 1)])
                ins.then_inc(s["qkv_ready"], 1)
                act.wait_ge(s["qkv_done"], b * 4 + 4)
                act.wait_ge(s["pv_done"], b * 4)
                for t in range(HALVES):
                    src = bank[5][:, t * H:(t + 1) * H].rearrange("p (n r d) -> p n r d", r=2, d=HD)
                    ins = nc.scalar.activation(vp[:, t, :, 0:4:3, :], src, ACT.Copy)
                ins.then_inc(s["qkv_ready"], 1)
                act.wait_ge(s["mt_done"], b + 1)
                nc.scalar.activation(mT[:, :], bank[1][:, 0:S], ACT.Copy).then_inc(s["mT_ready"], 1)
                for h in range(NH):
                    g = h // 4
                    act.wait_ge(s["st_done"], b * NH + (h + 1))
                    if h % 4 == 0:
                        act.wait_ge(s["pv_done"], b * 4 + max(g - 1, 0))
                    nc.scalar.activation(ex[:, g % 2, h % 4, :], bank[2 + (NH + h) % 6][:, :], ACT.Exp, scale=SCALE)\
                        .then_inc(s["exp_done"], 1)
            act.wait_ge(s["ld_l1"], 16 * 11)
            act.wait_ge(s["const_pool"], 2)
            act.wait_ge(s["x1_ready"], B)
            own = Own(act, s["act_own"])
            nc.scalar.activation(tA[:, :], tA[:, :], ACT.Tanh).then_inc(s["dt_out"], 1)
            with act.Fori(0, B) as b:
                own.enter(b, 1)
                act.wait_ge(s["xr_done"], b * 2 + 2)
                act.wait_ge(s["conv_done"], b)
                for c in range(CT):
                    ins = nc.scalar.activation(xrp[:, c, TAPS - 1:], bank[c // 2][:, (c % 2) * S:(c % 2 + 1) * S],
                                               ACT.Identity, bias=cond[:, c, bass.ds(b, 1)])
                ins.then_inc(s["xr_in"], 1)
                own.mark(nc.scalar.activation(sqj[:, 0:1], sqj[:, 0:1], ACT.Copy) if False else
                         nc.scalar.activation(nrm[:, 0:1], ones[:, 0:1], ACT.Copy))
                act.wait_ge(s["xr_in"], b + 1)
                for c in range(CT):
                    ins = nc.scalar.activation(acc[:, c, :], xrp[:, c, TAPS - 1:], ACT.Identity,
                                               bias=bcv[:, c:c + 1], scale=wcv[:, c, TAPS - 1:TAPS])
                ins.then_inc(s["tap3_ready"], 1)
                act.wait_ge(s["gate_done"], b * 2 + 2)
                for c2 in range(2):
                    ins = nc.scalar.activation(gateT[:, 2 * c2:2 * c2 + 2, bass.ds(b * S, S)],
                                               bank[2 + c2][:, :].rearrange("p (k s) -> p k s", k=2), ACT.Silu)
                ins.then_inc(s["gate_out"], 1)
                act.wait_ge(s["conv_done"], b + 1)
                act.wait_ge(s["xcT_used"], b)
                nc.scalar.activation(xcT[:, :, :], acc[:, :, :], ACT.Silu).then_inc(s["xcT_ready"], 1)
                for t in range(HALVES):
                    act.wait_ge(s["tok_ready"], b * HALVES + (t + 1))
                    nc.scalar.activation(xc[:, b * HALVES + t, :], bank[5 + t][:, :], ACT.Copy)\
                        .then_inc(s["tok_taken"], 1)
            own.leave(B)
            act.wait_ge(s["rt_in"], 3)
            nc.scalar.activation(rt[:, :], var_e[:, :], ACT.Sqrt).then_inc(s["rt_out"], 1)
            with act.Fori(0, B) as b:
                for t in range(HALVES):
                    act.wait_ge(s["xn_ready"], b * HALVES + (t + 1))
                    nc.scalar.activation(sqj[:, :], xn[:, t, :], ACT.Square, accum_out=ss[:, bass.ds(b * HALVES + t, 1)])\
                        .then_inc(s["sq_done"], 1)
                    act.wait_ge(s["xs_out"], b * (16 * HALVES) + 0)
                    nc.scalar.activation(xpart[:, t, 0, :], xn[:, t, :], ACT.Copy).then_inc(s["part0"], 1)
                    act.wait_ge(s["rem0"], b * HALVES + (t + 1))
                    nc.scalar.activation(xpart[:, t, 1, :], xrem[:, t, :], ACT.Copy).then_inc(s["part1"], 1)
            act.wait_ge(s["sq_done"], NT)
            nc.scalar.activation(nrm[:, :], ss[:, :], ACT.Sqrt).then_inc(s["nrm_ready"], 1)
            act.wait_ge(s["dt_in"], 1)
            nc.scalar.activation(dtt[:, :, :], dtt[:, :, :], ACT.Tanh).then_inc(s["dt_out"], 1)
            with act.Fori(0, NCH // 2) as i:
                for par in range(2):
                    act.wait_ge(s[f"yst{par}"], i * 64)
                    for g in range(CH // 4):
                        n = par * (CH // 4) + g
                        act.wait_ge(s["y_done"], i * (2 * CH // 4) + (n + 1))
                        nc.scalar.activation(yb[:, par, g, :], bank[4 + n % 2][:, :], ACT.Copy)\
                            .then_inc(s["y_taken"], 1)
            with act.Fori(0, B) as b:
                for t in range(HALVES):
                    act.wait_ge(s["o_done"], b * HALVES + (t + 1))
                    act.wait_ge(s["o_out"], b * (16 * HALVES))
                    nc.scalar.activation(ob[:, t, :], bank[6 + t][:, 0:H], ACT.Copy).then_inc(s["ob_ready"], 1)
                    act.wait_ge(s["ob_ready"], b * HALVES + (t + 1))
                    act.dma_start(out[b, t * P:(t + 1) * P, :], ob[:, t, :]).then_inc(s["o_out"], 16)
            act.wait_ge(s["o_out"], 16 * NT)

        @block.tensor
        def _(pe):
            mm = nc.tensor.matmul
            pe.wait_ge(s["dcsum"], 1)
            for w in range(5):
                for o in range(HT):
                    for k in range(HT):
                        st = cond2[:, (0 if w < 3 else HT) + k, :]
                        col = (w * HT + o) * B
                        ins = mm(bank[0][:, col:col + B], wsq[:, w, k, o * P:(o + 1) * P], st, start=k == 0,
                                 stop=k == HT - 1)
            ins.then_inc(s["dcsum"], 1)
            pe.wait_ge(s["ld_c"], 16 * 4)
            pe.wait_ge(s["dc_done"], 1)
            pe.wait_ge(s["const_pool"], 1)
            with pe.Fori(0, B) as b:
                pe.wait_ge(s["xnb_ready"], b + 1)
                pe.wait_ge(s["att_ready"], b)
                for k in range(HT):
                    for t in range(HALVES):
                        ins = nc.tensor.transpose(bank[0][:, k * S + t * P:k * S + (t + 1) * P],
                                                  xnb[:, t, k * P:(k + 1) * P], ident[:, :])
                ins.then_inc(s["tr_done"], 1)
                pe.wait_ge(s["xnT_ready"], b + 1)
                pe.wait_ge(s["x1_ready"], b)
                pe.wait_ge(s["exp_done"], b * NH)
                for w, bk in ((0, 2), (1, 3), (2, 4)):
                    for o in range(HT):
                        for k in range(HT):
                            ins = mm(bank[bk][:, o * S:(o + 1) * S], w5[:, w, k, o * P:(o + 1) * P], xnT[:, k, :],
                                     start=k == 0, stop=k == HT - 1)
                    ins.then_inc(s["qkv_done"], 1)
                for t in range(HALVES):
                    for k in range(HT):
                        ins = mm(bank[5][:, t * H:(t + 1) * H], xnT[:, k, t * P:(t + 1) * P], w5[:, 2, k, :],
                                 start=k == 0, stop=k == HT - 1)
                ins.then_inc(s["qkv_done"], 1)
                pe.wait_ge(s["qkv_ready"], b * 4 + 4)
                for g in range(4):
                    o, par = g // 2, g % 2
                    if g > 0:
                        pe.wait_ge(s["maxes"], b * NH + (4 * g - 2))
                    for t in range(HALVES):
                        for r in range(4):
                            rows = slice(32 * r, 32 * r + 32)
                            ins = mm(bank[2 + (4 * g + r) % 6][:, t * S:(t + 1) * S],
                                     qT[rows, o, t * P:(t + 1) * P], kT[rows, par, o, :], start=True, stop=True)
                            if t == HALVES - 1:
                                ins.then_inc(s["smax_done"], 1)
                pe.wait_ge(s["maxes"], b * NH + NH)
                for t in range(HALVES):
                    ins = nc.tensor.transpose(bank[1][:, t * P:(t + 1) * P], mx[:, t, :], ident[:, :])
                ins.then_inc(s["mt_done"], 1)
                pe.wait_ge(s["mT_ready"], b + 1)

                def scores(g):
                    o, par = g // 2, g % 2
                    if g > 0:
                        pe.wait_ge(s["exp_done"], b * NH + (4 * g - 2))
                    for t in range(HALVES):
                        for r in range(4):
                            rows = slice(32 * r, 32 * r + 32)
                            mm(bank[2 + (NH + 4 * g + r) % 6][:, t * S:(t + 1) * S],
                               kT[rows, par, o, t * P:(t + 1) * P], qT[rows, o, :], start=True, stop=False)
                        for r in range(4):
                            rows = slice(32 * r, 32 * r + 32)
                            ins = mm(bank[2 + (NH + 4 * g + r) % 6][:, t * S:(t + 1) * S],
                                     sel[rows, g, :], mT[rows, :], start=False, stop=True)
                            if t == HALVES - 1:
                                ins.then_inc(s["st_done"], 1)

                def weigh(g):
                    o, par = g // 2, g % 2
                    pe.wait_ge(s["exp_done"], b * NH + (4 * g + 4))
                    for bk in range(2):
                        for t in range(HALVES):
                            for r in range(4):
                                lhs = (vp[:, t, 4 * o + r, 2 * par:2 * par + 2, :].rearrange("p a d -> p (a d)")
                                       if bk == 0 else half_ones[:, par, :])
                                ins = mm(bank[bk][32 * r:32 * r + 32, o * S:(o + 1) * S], lhs,
                                         ex[:, g % 2, r, t * S:(t + 1) * S], start=par == 0 and t == 0,
                                         stop=par == 1 and t == HALVES - 1, skip_group_check=True)
                    ins.then_inc(s["pv_done"], 1)

                scores(0)
                scores(1)
                weigh(0)
                scores(2)
                weigh(1)
                scores(3)
                weigh(2)
                weigh(3)
                pe.wait_ge(s["exp_done"], b * NH + NH)
                pe.wait_ge(s["att_ready"], b + 1)
                for w, bk, src in ((4, 3, vT), (3, 2, attT)):
                    for o in range(HT):
                        for k in range(HT):
                            ins = mm(bank[bk][:, o * S:(o + 1) * S], w5[:, w, k, o * P:(o + 1) * P], src[:, k, :],
                                     start=k == 0, stop=k == HT - 1)
                ins.then_inc(s["wu_done"], 1)

            pe.wait_ge(s["ld_l1"], 16 * 11)
            pe.wait_ge(s["x1_ready"], B)
            for c in range(CT):
                ins = mm(bank[7][:, c * NS:(c + 1) * NS], wxd[:, c * P:(c + 1) * P], wdt[:, :], start=True, stop=True)
            ins.then_inc(s["wcomp"], 1)
            pe.wait_ge(s["wgain"], 1)
            for j, (lhs, rhs) in enumerate(((None, wxg), (lnb_rep, wx))):
                for c in range(CT):
                    ins = mm(bank[7][:, 64 + 64 * j:64 + 64 * j + NP3], ones[:, :] if lhs is None else lhs[:, c, :],
                             rhs[:, c, :], start=c == 0, stop=c == CT - 1)
            ins.then_inc(s["pconst"], 1)
            with pe.Fori(0, B) as b:
                for c in range(2 * CT):
                    if c == 0:
                        pe.wait_ge(s["xr_in"], b)
                    if c == CT:
                        pe.wait_ge(s["gate_out"], b)
                    for k in range(HT):
                        ins = mm(bank[c // 2][:, (c % 2) * S:(c % 2 + 1) * S], win[:, k, c * P:(c + 1) * P],
                                 xres[:, k, bass.ds(b * S, S)], start=k == 0, stop=k == HT - 1)
                    if c % 2:
                        ins.then_inc(s["xr_done"] if c < CT else s["gate_done"], 1)
                pe.wait_ge(s["xcT_ready"], b + 1)
                pe.wait_ge(s["tok_taken"], b * HALVES)
                for t in range(HALVES):
                    for c in range(CT):
                        ins = nc.tensor.transpose(bank[5 + t][:, c * P:(c + 1) * P], xcT[:, c, t * P:(t + 1) * P],
                                                  ident[:, :])
                    ins.then_inc(s["tok_ready"], 1)
                pe.wait_ge(s["raw_ready"], b)
                for t in range(HALVES):
                    for c in range(CT):
                        ins = mm(bank[4][:, t * 64:t * 64 + NP3], xcT[:, c, t * P:(t + 1) * P], wxg[:, c, :],
                                 start=c == 0, stop=c == CT - 1)
                ins.then_inc(s["xcT_used"], 1)
            pe.wait_ge(s["eb_ready"], 1)
            for j, src in enumerate((adt, cdt)):
                for t in range(HALVES):
                    ins = nc.tensor.transpose(bank[j][:, t * P:(t + 1) * P],
                                              src[:, t, :, :].rearrange("p b d -> p (b d)"), ident[:, :])
            ins.then_inc(s["eb_tr"], 1)
            pe.wait_ge(s["ipc_ready"], 1)
            for j, src in enumerate((ipc, dr)):
                for t in range(HALVES):
                    ins = nc.tensor.transpose(bank[2 + j][:, t * P:(t + 1) * P], src[:, t * P:(t + 1) * P],
                                              ident[:, :])
            ins.then_inc(s["eb_back"], 1)
            pe.wait_ge(s["bsplit"], 2)
            pe.wait_ge(s["c_ready"], 1)

            def u_steps(par, g, first, z_seen):
                for k in range(4):
                    step = 4 * g + k
                    if not first:
                        pe.wait_ge(s["z_ready"], z_seen + (step - 3))
                    mm(bank[k][:, :], bst[0:KU, par, step, :], xst[0:KU, par, step, :], start=True, stop=True)\
                        .then_inc(s["u_done"], 1)

            def y_steps(par, g, z_seen, y_seen):
                pe.wait_ge(s["z_ready"], z_seen + (4 * g + 4))
                pe.wait_ge(s["y_taken"], y_seen)
                for k in range(4):
                    step = 4 * g + k
                    ins = mm(bank[4 + g % 2][32 * k:32 * k + 32, :], cst[:, par, step, :], zst[:, step % ZR, :],
                             start=True, stop=True)
                ins.then_inc(s["y_done"], 1)

            G = CH // 4
            pe.wait_ge(s["ld_x0"], 16 * len(PAIRS))
            pe.wait_ge(s["ld_b0"], 16)
            u_steps(0, 0, True, 0)
            with pe.Fori(0, NCH // 2 - 1) as i:
                for n in range(2 * G):
                    par, g = n // G, n % G
                    nxt = (n + 1) % (2 * G)
                    if nxt % G == 0:
                        q = nxt // G
                        load = i + (2 if q == 0 else 1)
                        pe.wait_ge(s[f"ld_x{q}"], load * (16 * len(PAIRS)))
                        pe.wait_ge(s[f"ld_b{q}"], load * 16)
                    if nxt == 0:
                        u_steps(0, 0, False, i * (2 * CH) + 2 * CH)
                    else:
                        u_steps(nxt // G, nxt % G, False, i * (2 * CH) + (nxt // G) * CH)
                    if g == 0:
                        pe.wait_ge(s["cst_ready"], i * 2 + (par + 1))
                    y_steps(par, g, i * (2 * CH) + par * CH, i * (2 * G) + max(n - 1, 0))
            last = (NCH // 2 - 1)
            for n in range(2 * G):
                par, g = n // G, n % G
                if n + 1 < 2 * G:
                    if (n + 1) % G == 0:
                        pe.wait_ge(s["ld_x1"], (last + 1) * (16 * len(PAIRS)))
                        pe.wait_ge(s["ld_b1"], (last + 1) * 16)
                    u_steps((n + 1) // G, (n + 1) % G, False, last * 2 * CH + (n + 1) // G * CH)
                if g == 0:
                    pe.wait_ge(s["cst_ready"], last * 2 + par + 1)
                y_steps(par, g, last * 2 * CH + par * CH, last * 2 * G + max(n - 1, 0))
            pe.wait_ge(s["y_taken"], NCH * G)
            with pe.Fori(0, B) as b:
                pe.wait_ge(s["x1s_ready"], b + 1)
                for t in range(HALVES):
                    pe.wait_ge(s["ysum_ready"], b * HALVES + (t + 1))
                    pe.wait_ge(s["yg_ready"], b * HALVES + t)
                    for c in range(CT):
                        ins = nc.tensor.transpose(bank[4][:, c * P:(c + 1) * P], ysum[:, t, c * P:(c + 1) * P],
                                                  ident[:, :])
                    ins.then_inc(s["yt_done"], 1)
                    pe.wait_ge(s["yg_ready"], b * HALVES + (t + 1))
                    pe.wait_ge(s["ob_ready"], b * HALVES)
                    for c in range(CT):
                        mm(bank[6 + t][:, 0:H], yg[:, c, :], wo[:, c, :], start=c == 0, stop=False,
                           skip_group_check=True)
                    for k in range(HT):
                        ins = mm(bank[6 + t][:, k * P:(k + 1) * P], x1s[:, k, t * P:(t + 1) * P], ident[:, :],
                                 start=False, stop=k == HT - 1, skip_group_check=True)
                    ins.then_inc(s["o_done"], 1)

        @block.vector
        def _(dve):
            v = nc.vector
            own = Own(dve, s["vec"])

            def statistics(tiles):
                own.settle()
                for n in range(NT):
                    own.mark(v.bn_stats(bn[:, n, :], tiles[:, n, :]))
                own.settle()
                for n in range(NT):
                    own.mark(v.bn_aggr(mv[:, n, :], bn[:, n, :]))
                own.settle()

            v.memset(xst[32:64, :, :, :], 1.0).then_inc(s["xone_ready"], 1)
            dve.wait_ge(s["ld_w"], 32)
            v.tensor_tensor(wsq[:, :, :, :], w5[:, :, :, :], w5[:, :, :, :], ALU.mult)
            v.tensor_tensor(cond2[:, :, :], cond[:, :, :], cond[:, :, :], ALU.mult).then_inc(s["dcsum"], 1)
            dve.wait_ge(s["dcsum"], 2)
            v.tensor_scalar(dcv[:, :, :, :].rearrange("p w o b -> p (w o b)"), bank[0][:, 0:10 * B], EPS_DM, None,
                            ALU.add).then_inc(s["rt_in"], 1)
            dve.wait_ge(s["rt_out"], 1)

            def rsqrt(y, root, x, tmp):
                own.mark(v.reciprocal(y, root))
                own.settle()
                own.mark(v.tensor_tensor(tmp, y, y, ALU.mult))
                own.settle()
                own.mark(v.tensor_tensor(tmp, tmp, x, ALU.mult))
                own.settle()
                own.mark(v.tensor_scalar(tmp, tmp, -0.5, 1.5, ALU.mult, ALU.add))
                own.settle()
                own.mark(v.tensor_tensor(y, y, tmp, ALU.mult))
                own.settle()

            rsqrt(dc[:, :, :, :], dct[:, :, :, :], dcv[:, :, :, :], dct[:, :, :, :])
            dve.wait_ge(s["ld_c"], 16 * 4)
            for par in range(2):
                v.tensor_scalar(kdc[:, :, :, par].rearrange("p b o -> p o b"), dc[:, 1, :, :], parity[:, par:par + 1],
                                None, ALU.mult)
            own.mark(v.tensor_tensor(vdc[:, :, :], dc[:, 2, :, :], cond[:, HT:2 * HT, :], ALU.mult))
            own.settle()
            v.memset(tick[:, :], 0.0).then_inc(s["dc_done"], 1)
            dve.wait_ge(s["ld_l0"], 32)
            for n in range(NT):
                own.mark(v.tensor_tensor(xt[:, n, :], xt[:, n, :], s1b[:, n // HALVES, :], ALU.mult))
            statistics(xt)
            v.tensor_scalar(var_e[:, :], mv[:, :, 1], EPS_LN, None, ALU.add).then_inc(s["rt_in"], 1)
            dve.wait_ge(s["rt_in"], 2)
            dve.wait_ge(s["rt_out"], 2)
            rsqrt(rs[:, :], rt[:, :], var_e[:, :], rt[:, :])
            dve.wait_ge(s["ld_x"], 16)
            dve.wait_ge(s["const_pool"], 1)
            with dve.Fori(0, B) as b:
                own.enter(b, 3)
                dve.wait_ge(s["tr_done"], b)
                for t in range(HALVES):
                    ins = v.tensor_scalar(xnb[:, t, :], xt[:, b * HALVES + t, :], mv[:, b * HALVES + t, 0:1],
                                          rs[:, bass.ds(b * HALVES + t, 1)], ALU.subtract, ALU.mult)
                ins.then_inc(s["xnb_ready"], 1)
                dve.wait_ge(s["mt_done"], b)
                for h in range(NH):
                    g, r = h // 4, h % 4
                    dve.wait_ge(s["smax_done"], b * NH + (h + 1))
                    v.tensor_reduce(mx[:, :, 32 * r + g:32 * r + g + 1],
                                    bank[2 + h % 6][:, :].rearrange("p (t k) -> p t k", t=HALVES), AX.X, ALU.max)\
                        .then_inc(s["maxes"], 1)
                dve.wait_ge(s["pv_done"], b * 4 + 4)
                dve.wait_ge(s["wu_done"], b)
                own.mark(v.reciprocal(rec[:, :, :].rearrange("p o s -> p (o s)"), bank[1][:, :]))
                own.settle()
                for o in range(HT):
                    ins = v.scalar_tensor_tensor(attT[:, o, :], bank[0][:, o * S:(o + 1) * S],
                                                 vdc[:, o, bass.ds(b, 1)], rec[:, o, :], ALU.mult, ALU.mult)
                ins.then_inc(s["att_ready"], 1)
                dve.wait_ge(s["wu_done"], b + 1)
                for bk, w in ((2, 3), (3, 4)):
                    for o in range(HT):
                        tile = xres[:, o, bass.ds(b * S, S)]
                        ins = v.scalar_tensor_tensor(tile, bank[bk][:, o * S:(o + 1) * S], dc[:, w, o, bass.ds(b, 1)],
                                                     tile, ALU.mult, ALU.add)
                    if bk == 2:
                        own.mark(ins)
                        own.settle()
                own.mark(v.memset(tick[:, :], 0.0))
                ins.then_inc(s["x1_ready"], 1)
            own.leave(B)
            dve.wait_ge(s["ld_l1"], 16 * 11)
            dve.wait_ge(s["wcomp"], 1)
            own.mark(v.tensor_copy(wx[:, :, 2 * NS:], bank[7][:, 0:CT * NS].rearrange("p (c n) -> p c n", c=CT)))
            own.settle()
            for c in range(CT):
                v.tensor_scalar(wxg[:, c, :], wx[:, c, :], lnt[:, 0, c:c + 1], None, ALU.mult)
                ins = v.tensor_scalar(lnb_rep[:, c, :], ones[:, :], lnt[:, 1, c:c + 1], None, ALU.mult)
            ins.then_inc(s["wgain"], 1)
            dve.wait_ge(s["pconst"], 1)
            v.tensor_copy(proj_sum[:, :], bank[7][:, 64:64 + NP3])
            own.mark(v.tensor_copy(proj_off[:, :], bank[7][:, 128:128 + NP3]))
            own.settle()
            own.mark(v.tensor_tensor(proj_off[:, 2 * NS:], proj_off[:, 2 * NS:], bdt[:, :], ALU.add))
            own.settle()
            with dve.Fori(0, B) as b:
                own.enter(b, TAPS - 2)
                dve.wait_ge(s["tap3_ready"], b + 1)
                for k in range(TAPS - 1):
                    for c in range(CT):
                        ins = v.scalar_tensor_tensor(acc[:, c, :], xrp[:, c, k:k + S], wcv[:, c, k:k + 1],
                                                     acc[:, c, :], ALU.mult, ALU.add)
                    if k < TAPS - 2:
                        own.mark(ins)
                        own.settle()
                ins.then_inc(s["conv_done"], 1)
                dve.wait_ge(s["xcT_used"], b + 1)
                v.tensor_copy(raw[:, bass.ds(b * HALVES, HALVES), :],
                              bank[4][:, 0:2 * 64].rearrange("p (t n) -> p t n", t=HALVES)[:, :, 0:NP3])\
                    .then_inc(s["raw_ready"], 1)
            own.leave(B)
            dve.wait_ge(s["tok_taken"], NT)
            statistics(xc)
            v.tensor_scalar(var_e[:, :], mv[:, :, 1], EPS_LN, None, ALU.add).then_inc(s["rt_in"], 1)
            dve.wait_ge(s["rt_in"], 3)
            dve.wait_ge(s["rt_out"], 3)
            rsqrt(rs[:, :], rt[:, :], var_e[:, :], rt[:, :])
            with dve.Fori(0, B) as b:
                own.enter(b, 2 * HALVES)
                for t in range(HALVES):
                    n = b * HALVES + t
                    dve.wait_ge(s["sq_done"], b * HALVES)
                    dve.wait_ge(s["dx_ready"], b * HALVES)
                    own.mark(v.tensor_scalar(xn[:, t, :], xc[:, n, :], mv[:, n, 0:1], rs[:, bass.ds(n, 1)],
                                             ALU.subtract, ALU.mult))
                    own.settle()
                    own.mark(v.tensor_tensor(xn[:, t, :], xn[:, t, :], lnr[:, 0, :], ALU.mult))
                    own.settle()
                    v.tensor_tensor(xn[:, t, :], xn[:, t, :], lnr[:, 1, :], ALU.add).then_inc(s["xn_ready"], 1)
                    dve.wait_ge(s["part0"], b * HALVES + (t + 1))
                    dve.wait_ge(s["xn_ready"], b * HALVES + (t + 1))
                    v.tensor_tensor(xrem[:, t, :], xn[:, t, :], xpart[:, t, 0, :], ALU.subtract)\
                        .then_inc(s["rem0"], 1)
                    dve.wait_ge(s["part1"], b * HALVES + (t + 1))
                    dve.wait_ge(s["rem0"], b * HALVES + (t + 1))
                    v.tensor_tensor(xpart[:, t, 2, :], xrem[:, t, :], xpart[:, t, 1, :], ALU.subtract)\
                        .then_inc(s["parts_ready"], 1)
            own.leave(B)
            def wide(ap):
                return ap.unsqueeze(2).broadcast_to([P, NT, NP3])

            def rows(ap):
                return ap.unsqueeze(1).broadcast_to([P, NT, ap.shape[1]])

            own.mark(v.tensor_tensor(raw[:, :, :], raw[:, :, :], wide(rs[:, :]), ALU.mult))
            own.mark(v.tensor_tensor(var_e[:, :], mv[:, :, 0], rs[:, :], ALU.mult))
            own.settle()
            own.mark(v.tensor_tensor(t48[:, :, :], wide(var_e[:, :]), rows(proj_sum[:, :]), ALU.mult))
            own.settle()
            own.mark(v.tensor_tensor(raw[:, :, :], raw[:, :, :], t48[:, :, :], ALU.subtract))
            own.settle()
            own.mark(v.tensor_tensor(raw[:, :, :], raw[:, :, :], rows(proj_off[:, :]), ALU.add))
            own.settle()
            v.tensor_copy(dtt[:, :, :], raw[:, :, 2 * NS:]).then_inc(s["dt_in"], 1)
            dve.wait_ge(s["nrm_ready"], 1)
            own.mark(v.tensor_scalar(nrm[:, :], nrm[:, :], 1.0, None, ALU.min))
            own.settle()
            own.mark(v.tensor_tensor(bnt[:, :, :, :].rearrange("p t b d -> p b t d"),
                                     raw[:, :, 0:NS].rearrange("p (b t) d -> p b t d", t=HALVES),
                                     nrm[:, :].rearrange("p (b t) -> p b t", t=HALVES).unsqueeze(3)
                                     .broadcast_to([P, B, HALVES, NS]), ALU.mult))
            own.mark(v.tensor_copy(cdt[:, :, :, :].rearrange("p t b d -> p b t d"),
                                   raw[:, :, NS:2 * NS].rearrange("p (b t) d -> p b t d", t=HALVES)))
            own.mark(v.tensor_reduce(ybias[:, :].unsqueeze(2), raw[:, :, NS:2 * NS], AX.X, ALU.add))
            own.settle()
            own.mark(v.tensor_scalar(ybias[:, :], ybias[:, :], -BOUND, None, ALU.mult))
            dve.wait_ge(s["dt_out"], 2)
            own.mark(v.tensor_tensor(dtt[:, :, :], dtt[:, :, :], rows(tA[:, :]), ALU.mult))
            own.settle()
            v.tensor_scalar(adt[:, :, :, :].rearrange("p t b d -> p b t d"),
                            dtt[:, :, :].rearrange("p (b t) d -> p b t d", t=HALVES), -STEP, 1.0, ALU.mult, ALU.add)\
                .then_inc(s["eb_ready"], 1)
            dve.wait_ge(s["eb_tr"], 1)
            own.mark(v.tensor_tensor_scan(pcum[:, :], bank[0][:, 0:S], one_row[:, :], 1.0, ALU.mult, ALU.mult))
            own.settle()
            own.mark(v.reciprocal(ipc[:, :], pcum[:, :]))
            own.mark(v.tensor_tensor(cP[:, :], bank[1][:, 0:S], pcum[:, :], ALU.mult))
            own.settle()
            own.mark(v.tensor_scalar(rr[:, 1:], ipc[:, :], BOUND, None, ALU.mult))
            own.mark(v.tensor_scalar(hi[:, :], ipc[:, :], 2 * BOUND, None, ALU.mult))
            own.settle()
            v.tensor_tensor(dr[:, :], rr[:, 1:], rr[:, 0:S], ALU.subtract).then_inc(s["ipc_ready"], 1)
            v.memset(tick[:, :], 0.0).then_inc(s["c_ready"], 1)
            dve.wait_ge(s["eb_back"], 1)

            def split(parts, rem):
                flat = [parts[:, k, :, :].rearrange("p t n -> p (t n)") for k in range(3)]
                r = rem[:, :, :].rearrange("p t n -> p (t n)")
                for k in range(2):
                    own.mark(v.tensor_copy(flat[k], r))
                    own.settle()
                    own.mark(v.tensor_tensor(r, r, flat[k], ALU.subtract))
                    own.settle()
                v.tensor_copy(flat[2], r).then_inc(s["bsplit"], 1)

            own.mark(v.tensor_tensor(brem[:, :, :].rearrange("p t n -> p (t n)"), bank[2][:, 0:S],
                                     bnt[:, :, :, :].rearrange("p t b d -> p (t b d)"), ALU.mult))
            own.settle()
            split(bpart, brem)
            own.mark(v.tensor_copy(drem[:, :, :].rearrange("p t n -> p (t n)"), bank[3][:, 0:S]))
            own.settle()
            split(dpart, drem)
            for t in range(S):
                dve.wait_ge(s["u_done"], t + 1)
                if t > 0:
                    dve.wait_ge(s["z_ready"], t)
                if t % 4 == 0 and t >= ZR:
                    dve.wait_ge(s["y_done"], (t - ZR) // 4 + 1)
                v._custom_dve(bass.dve_ops.TENSOR_ADD_SAT, out=zst[:, t % ZR, :], in0=zst[:, (t - 1) % ZR, :],
                              in1=bank[t % 4][:, :], s0=hi[:, t:t + 1], s1=0.0).then_inc(s["z_ready"], 1)
            with dve.Fori(0, B) as b:
                for t in range(HALVES):
                    n = b * HALVES + t
                    dve.wait_ge(s[f"ld_y{t}"], b * 16 + 16)
                    dve.wait_ge(s["yt_done"], b * HALVES)
                    v.scalar_tensor_tensor(ysum[:, t, :], ytk[:, t, :], ybias[:, bass.ds(n, 1)], xc[:, n, :],
                                           ALU.add, ALU.add).then_inc(s["ysum_ready"], 1)
                    dve.wait_ge(s["yt_done"], b * HALVES + (t + 1))
                    dve.wait_ge(s["o_done"], b * HALVES + t)
                    v.tensor_tensor(yg[:, :, :], bank[4][:, :].rearrange("p (c s) -> p c s", c=CT),
                                    gateT[:, :, bass.ds(b * S + t * P, P)], ALU.mult).then_inc(s["yg_ready"], 1)


def kernel(x, cond_2048, L0_cond_q_weight, L0_cond_k_weight, L0_cond_v_weight, L0_cond_w_weight, L0_cond_u_weight,
           L1_cond_W_in, L1_cond_W_conv, L1_cond_b_conv, L1_cond_ln_g, L1_cond_ln_b, L1_cond_W_xproj, L1_cond_W_dt,
           L1_cond_b_dt, L1_cond_A_log, L1_cond_D, L1_cond_W_out):
    import concourse.bacc as bacc
    from concourse.bass_utils import run_bass_kernel_spmd

    def channels(a, width):
        return np.asarray(a).reshape(-1, P, width).transpose(1, 0, 2)

    x, cond = np.asarray(x), np.asarray(cond_2048)
    w5 = np.stack([channels(np.asarray(w).T, H) for w in (L0_cond_q_weight, L0_cond_k_weight, L0_cond_v_weight,
                                                          L0_cond_w_weight, L0_cond_u_weight)], axis=1)
    per_channel = [np.asarray(a).reshape(CT, P).T for a in (L1_cond_ln_g, L1_cond_ln_b)]
    p = np.arange(P)
    pick = np.zeros((P, 4, P), np.float32)
    for g in range(4):
        pick[p % 32 == g, g, :] = -1.0
    arrays = {
        "x_tok": x.reshape(NT, P, H).transpose(1, 0, 2),
        "xT": channels(x.reshape(B * S, H).T, B * S),
        "s1_row": cond[:, :H],
        "condT": channels(cond.T, B),
        "w5T": w5,
        "winT": channels(np.asarray(L1_cond_W_in).T, 2 * C),
        "wconv": np.asarray(L1_cond_W_conv).reshape(CT, P, TAPS).transpose(1, 0, 2),
        "bconv": np.asarray(L1_cond_b_conv).reshape(CT, P).T,
        "ln_row": np.stack([np.asarray(a) for a in (L1_cond_ln_g, L1_cond_ln_b, L1_cond_D)]),
        "lnT": np.stack(per_channel, axis=1),
        "wxT": channels(np.asarray(L1_cond_W_xproj).T, NP3),
        "wxdt": np.asarray(L1_cond_W_xproj)[2 * NS:],
        "wdtT": np.asarray(L1_cond_W_dt).T,
        "bdt_row": np.asarray(L1_cond_b_dt),
        "alog_row": np.asarray(L1_cond_A_log),
        "woT": channels(np.asarray(L1_cond_W_out).T, H),
        "ident_d": np.eye(P, dtype=np.float32),
        "mask8_d": (p[:, None] // NS == np.arange(B)).astype(np.float32),
        "sel_d": pick,
        "parity_d": (p[:, None] // HD % 2 == np.arange(2)).astype(np.float32),
    }
    arrays = {k: np.ascontiguousarray(a) for k, a in arrays.items()}
    nc = bacc.Bacc("TRN2", target_bir_lowering=False, num_devices=1)
    aps = {k: nc.dram_tensor(k, a.shape, mybir.dt.from_np(a.dtype), kind="ExternalInput").ap()
           for k, a in arrays.items()}
    out = nc.dram_tensor("out", (B, S, H), F32, kind="ExternalOutput").ap()
    build(nc, *aps.values(), out)
    r = run_bass_kernel_spmd(nc, [arrays], core_ids=[0])
    return r.results[0]["out"]
```

```python
from contextlib import ExitStack

import numpy as np

import concourse.bass as bass
from concourse import mybir

F32 = mybir.dt.float32
BF16 = mybir.dt.bfloat16
ALU = mybir.AluOpType
ACT = mybir.ActivationFunctionType
AX = mybir.AxisListType

P = 128
B, S, H = 8, 256, 256
NH, HD = 16, 16
C, NS = 512, 16
TAPS = 4
HALVES = S // P
NT = B * HALVES
HT, CT = H // P, C // P
BOUND = 10.0
STEP = 0.01
SCALE = float(HD) ** -0.5
EPS_LN, EPS_DM = 1e-5, 1e-8
NP3 = 3 * NS
PAIRS = [(0, 0), (1, 0), (2, 0), (0, 1), (1, 1), (0, 2)]
KX = len(PAIRS) * B
KU = KX + 3
CH = 8
NCH = S // CH
HEADS = [2 * (2 * r + par) + o for o in range(HT) for par in range(2) for r in range(4)]
BD_J = B * (S * P)


class Own:

    def __init__(self, eng, sem):
        self.eng, self.sem, self.base, self.n, self.start = eng, sem, 0, 0, 0

    def enter(self, i, per):
        self.start += self.n
        self.n, self.per = 0, per
        self.base = i * per + self.start

    def leave(self, trips):
        assert self.n == self.per, (self.n, self.per)
        self.start += trips * self.per
        self.base, self.n = self.start, 0

    def mark(self, ins):
        ins.then_inc(self.sem, 1)
        self.n += 1

    def settle(self, back=0):
        self.eng.wait_ge(self.sem, self.base + self.n - back)


def build(nc, x_tok, xT, s1_row, condT, w5T, winT, wconv, bconv, ln_row, lnT, wxT, wxdt, wdtT, bdt_row, alog_row,
          woT, ident_d, mask8_d, out):
    with ExitStack() as ctx:
        def sb(name, shape, dt=F32):
            return ctx.enter_context(nc.sbuf_tensor(name, shape, dt))

        def sem(name):
            return ctx.enter_context(nc.semaphore(name))

        xs_d = nc.dram_tensor("xs_d", (3, B, S, C), BF16, kind="Internal").ap()
        bd_d = nc.dram_tensor("bd_d", (KU * S * P + 2 * B * NS,), BF16, kind="Internal").ap()
        qk_d = nc.dram_tensor("qk_d", (2, 2, 3, HD, NH, S), BF16, kind="Internal").ap()
        y_d = nc.dram_tensor("y_d", (S, B, C), F32, kind="Internal").ap()

        bank = [ctx.enter_context(nc.psum_tensor(f"bank{i}", [P, 512], F32)) for i in range(8)]

        ident = sb("ident", [P, P])
        mask8 = sb("mask8", [P, B])
        ones = sb("ones", [P, P])
        cond = sb("cond", [P, CT, B])
        w5 = sb("w5", [P, 5, HT, H])
        win = sb("win", [P, HT, 2 * C])
        wcv = sb("wcv", [P, CT, TAPS])
        bcv = sb("bcv", [P, CT])
        lnt = sb("lnt", [P, 2, CT])
        lnr = sb("lnr", [P, 3, C])
        wx = sb("wx", [P, CT, NP3])
        wxg = sb("wxg", [P, CT, NP3])
        wxd = sb("wxd", [NS, C])
        wdt = sb("wdt", [NS, NS])
        bdt = sb("bdt", [P, NS])
        tA = sb("tA", [P, NS])
        wo = sb("wo", [P, CT, H])
        lnb_rep = sb("lnb_rep", [P, CT, P])
        proj_sum = sb("proj_sum", [P, NP3])
        proj_off = sb("proj_off", [P, NP3])
        cond2 = sb("cond2", [P, CT, B])
        dc = sb("dc", [P, 5, HT, B])
        dcv = sb("dcv", [P, 5, HT, B])
        dct = sb("dct", [P, 5, HT, B])
        vdc = sb("vdc", [P, HT, B])
        half_ones = sb("half_ones", [P, 2, 2 * HD])

        xres = sb("xres", [P, HT, B * S])
        raw = sb("raw", [P, NT, NP3])
        mv = sb("mv", [P, NT, 2])
        bn = sb("bn", [P, NT, 6])
        tick = sb("tick", [P, 1])
        var_e = sb("var_e", [P, NT])
        rt = sb("rt", [P, NT])
        rs = sb("rs", [P, NT])
        ybias = sb("ybias", [P, NT])

        hi = sb("hi", [P, S])
        cP = sb("cP", [P, S])
        l0 = ExitStack()

        def sb0(name, shape, dt=F32):
            return l0.enter_context(nc.sbuf_tensor(name, shape, dt))

        xt = sb0("xt", [P, NT, H])
        s1b = sb0("s1b", [P, B, H])
        wsq = sb0("wsq", [P, 5, HT, H])
        xnb = sb0("xnb", [P, HALVES, H])
        xnT = sb0("xnT", [P, HT, S])
        qk = sb0("qk", [P, 2, HT * S])
        part = sb0("part", [P, 2, 3, HT * S], BF16)
        qst = sb0("qst", [P, 2, NH, S], BF16)
        kst = sb0("kst", [P, 2, NH, S], BF16)
        vT = sb0("vT", [P, HT, B * S])
        vp = sb0("vp", [P, HALVES, NH // 2, 4, HD])
        mx = sb0("mx", [P, HALVES, NH])
        mT = sb0("mT", [NH, S], BF16)
        ex = sb0("ex", [P, 2, 4, 512])
        rec = sb0("rec", [P, HT, S])
        attT = sb0("attT", [P, HT, S])
        l0.close()
        ZR = 8
        zst = sb("zst", [P, ZR, C])
        cst = sb("cst", [P, 2, CH, 32])
        xst = sb("xst", [P, 2, CH, C], BF16)
        bst = sb("bst", [P, 2, CH, P], BF16)
        yb = sb("yb", [P, 2, CH // 4, C])
        gateT = sb("gateT", [P, CT, B * S])
        xc = sb("xc", [P, NT, C])
        l1 = ExitStack()

        def sb1(name, shape, dt=F32):
            return l1.enter_context(nc.sbuf_tensor(name, shape, dt))

        ss = sb1("ss", [P, NT])
        shift = sb1("shift", [P, NT])
        nrm = sb1("nrm", [P, NT])
        t48 = sb1("t48", [P, NT, NP3])
        adt = sb1("adt", [P, HALVES, B, NS])
        cdt = sb1("cdt", [P, HALVES, B, NS])
        bnt = sb1("bnt", [P, HALVES, B, NS])
        dtt = sb1("dtt", [P, NT, NS])
        pcum = sb1("pcum", [P, S])
        one_row = sb1("one_row", [P, S])
        ipc = sb1("ipc", [P, S])
        rr = sb1("rr", [P, S + 1])
        dr = sb1("dr", [P, S])
        bpart = sb1("bpart", [P, 3, HALVES, B * NS], BF16)
        dpart = sb1("dpart", [P, 3, HALVES, B * NS], BF16)
        brem = sb1("brem", [P, HALVES, B * NS])
        drem = sb1("drem", [P, HALVES, B * NS])
        zeros = sb1("zeros", [P, 2048], BF16)
        conv_bufs = ExitStack()

        def sbc(name, shape, dt=F32):
            return conv_bufs.enter_context(nc.sbuf_tensor(name, shape, dt))

        xrp = sbc("xrp", [P, CT, TAPS - 1 + S])
        acc = sbc("acc", [P, CT, S])
        xcT = sbc("xcT", [P, CT, S])
        conv_bufs.close()
        xpart = sb1("xpart", [P, 2, 3, C], BF16)
        xrem = sb1("xrem", [P, 2, C])
        xn = sb1("xn", [P, 2, C])
        xz = sb1("xz", [P, 2, C])
        l1.close()
        ytk = sb("ytk", [P, 2, C])
        ysum = sb("ysum", [P, 2, C])
        yg = sb("yg", [P, CT, P])
        x1s = sb("x1s", [P, HT, S])
        ob = sb("ob", [P, 2, H])

        names = """ld_l0 ld_w ld_mod ld_x ld_l1 ld_c zfill vec act_own pool_own const_pool dcsum dc_done rt_in rt_out
            xnb_ready tr_done xnT_ready q_done k_done vt_done v_done q_in k_in vt_in v_in cast0 rem_qk cast1
            part_ready pw_q pw_k ld_q0 ld_q1 ld_k0 ld_k1 m_row
            smax_done maxes mt_done mT_ready st_done exp_done pv_done att_ready wu_done x1_ready wcomp wgain pconst xr_done xr_in tap3_ready gate_done gate_out conv_done
            conv_used xcT_ready xcT_used bcd_done raw_ready tok_ready tok_taken stats_ready xn_ready sq_done part0 part1
            rem0 rem1 parts_ready parts_out xs_out dx_ready ss_ready nrm_ready dt_in dt_out eb_ready eb_tr ipc_ready
            eb_back bsplit bd_out c_ready ld_x0 ld_b0 ld_x1 ld_b1 u_done z_ready y_done y_taken yst0 yst1 cst_ready ld_y0 ld_y1
            ysum_ready yt_done yg_ready o_done ob_ready o_out x1s_ready xz_ready shift_ready""".split()
        s = {n: sem(n) for n in names}

        block = ctx.enter_context(nc.Block())

        @block.sync
        def _(sp):
            for dst, src in ((xt[:, :, :], x_tok), (s1b[:, :, :], s1_row.partition_broadcast(P))):
                sp.dma_start(dst, src).then_inc(s["ld_l0"], 16)
            for dst, src in ((w5[:, :, :, :], w5T), (cond[:, :, :], condT)):
                sp.dma_start(dst, src).then_inc(s["ld_w"], 16)
            for dst, src in ((ident[:, :], ident_d), (mask8[:, :], mask8_d)):
                sp.dma_start(dst, src).then_inc(s["ld_c"], 16)
            sp.dma_start(xres[:, :, :], xT).then_inc(s["ld_x"], 16)
            for dst, src in ((win[:, :, :], winT), (wcv[:, :, :], wconv), (bcv[:, :], bconv), (lnt[:, :, :], lnT),
                             (lnr[:, :, :], ln_row.partition_broadcast(P)), (wx[:, :, :], wxT), (wxd[:, :], wxdt),
                             (wdt[:, :], wdtT), (bdt[:, :], bdt_row.partition_broadcast(P)),
                             (tA[:, :], alog_row.partition_broadcast(P)), (wo[:, :, :], woT)):
                sp.dma_start(dst, src).then_inc(s["ld_l1"], 16)

            def stack(b, par, turn, first):
                for w, name in enumerate("qk"):
                    sp.wait_ge(s["part_ready"], b * 2 + (w + 1))
                    if not first:
                        sp.wait_ge(s[f"ld_{name}{par}"], turn * 48)
                    for hh in range(NH // HT):
                        sp.dma_start(qk_d[par, w, :, :, hh * HT:(hh + 1) * HT, :].rearrange("k d h s -> d k (h s)"),
                                     part[hh * HD:(hh + 1) * HD, w, :, :]).then_inc(s[f"pw_{name}"], 16)
                for w, name, st in ((0, "q", qst), (1, "k", kst)):
                    sp.wait_ge(s[f"pw_{name}"], b * (16 * NH // HT) + 16 * NH // HT)
                    if not first:
                        sp.wait_ge(s["st_done"], b * NH - NH)
                    at = 0
                    for run in (3, 2, 1):
                        src = qk_d[par, w, 0:run] if w == 0 else qk_d[par, w, 3 - run:3]
                        sp.dma_start(st[at:at + run * HD, par, :, :], src.rearrange("k d h s -> (k d) h s"))\
                          .then_inc(s[f"ld_{name}{par}"], 16)
                        at += run * HD

            stack(0, 0, 0, True)
            stack(1, 1, 0, True)
            with sp.Fori(0, B // 2 - 1) as i:
                for k in range(2):
                    stack(i * 2 + (k + 2), k, i + 1, False)
            sp.wait_ge(s["bsplit"], 1)
            sp.wait_ge(s["zfill"], 16)
            for k in range(3):
                row = bd_d[(KX + k) * S * P:(KX + k + 1) * S * P].rearrange("(t c) -> t c", c=P)
                for t in range(HALVES):
                    sp.dma_start(row[t * P:(t + 1) * P], dpart[:, k, t, :]).then_inc(s["bd_out"], 16)
            with sp.Fori(0, B) as b:
                for t in range(HALVES):
                    sp.wait_ge(s["parts_ready"], b * HALVES + (t + 1))
                    sp.dma_start(xs_d[:, b, t * P:(t + 1) * P, :].rearrange("k p c -> p k c"), xpart[:, t, :, :])\
                      .then_inc(s["xs_out"], 16)
            sp.wait_ge(s["bsplit"], 2)
            for j, (_, bp) in enumerate(PAIRS):
                rows = bd_d[j * BD_J:j * BD_J + B * (S * P + NS)].rearrange("(b q) -> b q", b=B)[:, 0:S * P]
                rows = rows.rearrange("b (t c) -> t b c", c=P)[:, :, 0:NS]
                for t in range(HALVES):
                    sp.dma_start(rows[t * P:(t + 1) * P], bpart[:, bp, t, :].rearrange("p (b d) -> p b d", b=B))\
                      .then_inc(s["bd_out"], 16)
            n_bd = (len(PAIRS) + 3) * HALVES
            sp.wait_ge(s["xs_out"], 16 * NT)
            sp.wait_ge(s["bd_out"], 16 * n_bd)
            bd_v = bd_d[0:KU * S * P].rearrange("(k t c) -> k t c", t=S, c=P)

            def load_chunk(par, ch):
                t0 = ch * CH
                at = 0
                for run in (3, 2, 1):
                    for k in range(run):
                        sp.dma_start(xst[at:at + B, par, :, :], xs_d[k, :, bass.ds(t0, CH), :])\
                          .then_inc(s[f"ld_x{par}"], 16)
                        at += B
                sp.dma_start(bst[0:KU, par, :, :], bd_v[:, bass.ds(t0, CH), :]).then_inc(s[f"ld_b{par}"], 16)

            def store_chunk(par, ch):
                for k in range(4):
                    sp.dma_start(y_d[bass.ds(ch * CH, CH), :, :].rearrange("(g k) b c -> k b g c", k=4)[k],
                                 yb[32 * k:32 * k + B, par, :, :]).then_inc(s[f"yst{par}"], 16)

            sp.wait_ge(s["const_pool"], 2)
            load_chunk(0, 0)
            load_chunk(1, 1)
            with sp.Fori(0, NCH // 2 - 1) as i:
                for par in range(2):
                    sp.wait_ge(s["u_done"], i * (2 * CH) + (par + 1) * CH)
                    load_chunk(par, i * 2 + (par + 2))
                for par in range(2):
                    sp.wait_ge(s["y_taken"], i * (2 * CH // 4) + (par + 1) * (CH // 4))
                    store_chunk(par, i * 2 + par)
            for par in range(2):
                sp.wait_ge(s["y_taken"], (NCH // 2 - 1) * (2 * CH // 4) + (par + 1) * (CH // 4))
                store_chunk(par, NCH - 2 + par)
            sp.wait_ge(s["yst0"], NCH // 2 * 64)
            sp.wait_ge(s["yst1"], NCH // 2 * 64)
            for t in range(HALVES):
                sp.dma_start(ytk[:, t, :], y_d[t * P:(t + 1) * P, 0, :]).then_inc(s[f"ld_y{t}"], 16)
            with sp.Fori(0, B - 1) as b:
                for t in range(HALVES):
                    sp.wait_ge(s["ysum_ready"], b * HALVES + (t + 1))
                    sp.dma_start(ytk[:, t, :], y_d[t * P:(t + 1) * P, b + 1, :]).then_inc(s[f"ld_y{t}"], 16)

        @block.gpsimd
        def _(pool):
            own = Own(pool, s["pool_own"])
            own.mark(nc.gpsimd.memset(kst[96:P, :, :, :], -1.0))
            own.settle()
            nc.gpsimd.memset(vp[:, :, :, :, :], 0.0)
            nc.gpsimd.memset(half_ones[:, :, :], 0.0)
            own.mark(nc.gpsimd.memset(ones[:, :], 1.0))
            own.settle()
            nc.gpsimd.memset(half_ones[:, 0, 0:HD], 1.0)
            nc.gpsimd.memset(half_ones[:, 1, HD:2 * HD], 1.0).then_inc(s["const_pool"], 1)
            with pool.Fori(0, B) as b:
                for w in range(2):
                    pool.wait_ge(s["cast0"], b * 2 + (w + 1))
                    nc.gpsimd.tensor_tensor(qk[:, w, :], qk[:, w, :], part[:, w, 2 * w, :], ALU.subtract)\
                        .then_inc(s["rem_qk"], 1)
                for w in range(2):
                    pool.wait_ge(s["cast1"], b * 2 + (w + 1))
                    nc.gpsimd.tensor_tensor(part[:, w, 2 - 2 * w, :], qk[:, w, :], part[:, w, 1, :], ALU.subtract)\
                        .then_inc(s["part_ready"], 1)
            pool.wait_ge(s["x1_ready"], B)
            nc.gpsimd.memset(xst[:, :, :, :], 1.0)
            nc.gpsimd.memset(bst[:, :, :, :], 0.0)
            nc.gpsimd.memset(cst[:, :, :, :], 0.0)
            nc.gpsimd.memset(xrp[:, :, 0:TAPS - 1], 0.0)
            nc.gpsimd.memset(rr[:, 0:1], BOUND)
            nc.gpsimd.memset(zst[:, ZR - 1, :], BOUND)
            own.mark(nc.gpsimd.memset(zeros[:, :], 0.0))
            own.settle()
            nc.gpsimd.memset(one_row[:, :], 1.0).then_inc(s["const_pool"], 1)
            pool.dma_start(bd_d[0:KX * S * P].rearrange("(p r z) -> p r z", p=P, z=2048),
                           zeros[:, :].unsqueeze(1).broadcast_to([P, KX * S * P // (P * 2048), 2048]))\
                .then_inc(s["zfill"], 16)
            with pool.Fori(0, B) as b:
                for t in range(HALVES):
                    pool.wait_ge(s["xn_ready"], b * HALVES + (t + 1))
                    nc.gpsimd.tensor_tensor(xc[:, b * HALVES + t, :], xn[:, t, :], lnr[:, 2, :], ALU.mult)\
                        .then_inc(s["dx_ready"], 1)
                for t in range(HALVES):
                    pool.wait_ge(s["part1"], b * HALVES + (t + 1))
                    nc.gpsimd.tensor_tensor(xpart[:, t, 2, :], xrem[:, t, :], xpart[:, t, 1, :], ALU.subtract)\
                        .then_inc(s["parts_ready"], 1)
            pool.wait_ge(s["c_ready"], 1)
            def fill_chunk(par, ch):
                nc.gpsimd.tensor_tensor(cst[:, par, :, 0:B],
                                        cP[:, bass.ds(ch * CH, CH)].unsqueeze(2).broadcast_to([P, CH, B]),
                                        mask8[:, :].unsqueeze(1).broadcast_to([P, CH, B]), ALU.mult)\
                    .then_inc(s["cst_ready"], 1)

            fill_chunk(0, 0)
            fill_chunk(1, 1)
            with pool.Fori(0, NCH // 2 - 1) as i:
                for par in range(2):
                    pool.wait_ge(s["y_done"], i * (2 * CH // 4) + (par + 1) * (CH // 4))
                    fill_chunk(par, i * 2 + (par + 2))
            with pool.Fori(0, B) as b:
                pool.wait_ge(s["o_done"], b * HALVES)
                nc.gpsimd.tensor_copy(x1s[:, :, :], xres[:, :, bass.ds(b * S, S)]).then_inc(s["x1s_ready"], 1)

        @block.scalar
        def _(act):
            act.wait_ge(s["rt_in"], 1)
            nc.scalar.activation(dct[:, :, :, :], dcv[:, :, :, :], ACT.Sqrt).then_inc(s["rt_out"], 1)
            act.wait_ge(s["rt_in"], 2)
            nc.scalar.activation(rt[:, :], var_e[:, :], ACT.Sqrt).then_inc(s["rt_out"], 1)
            act.wait_ge(s["dc_done"], 1)
            act.wait_ge(s["const_pool"], 1)

            def take_qkv(b, first):
                act.wait_ge(s["tr_done"], b + 1)
                if not first:
                    act.wait_ge(s["v_done"], b)
                nc.scalar.activation(xnT[:, :, :], bank[0][:, :].rearrange("p (k s) -> p k s", k=HT), ACT.Copy)\
                    .then_inc(s["xnT_ready"], 1)
                for w, name in enumerate("qk"):
                    act.wait_ge(s[f"{name}_done"], b + 1)
                    if not first:
                        act.wait_ge(s["part_ready"], b * 2)
                        act.wait_ge(s[f"pw_{name}"], b * (16 * NH // HT))
                    for o in range(HT):
                        ins = nc.scalar.activation(qk[:, w, o * S:(o + 1) * S], bank[1 + w][:, o * S:(o + 1) * S],
                                                   ACT.Copy, scale=dc[:, w, o, bass.ds(b, 1)])
                    ins.then_inc(s[f"{name}_in"], 1)
                    act.wait_ge(s[f"{name}_in"], b + 1)
                    nc.scalar.activation(part[:, w, 2 * w, :], qk[:, w, :], ACT.Copy).then_inc(s["cast0"], 1)
                act.wait_ge(s["vt_done"], b + 1)
                for o in range(HT):
                    ins = nc.scalar.activation(vT[:, o, bass.ds(b * S, S)], bank[3][:, o * S:(o + 1) * S], ACT.Copy,
                                               scale=vdc[:, o, bass.ds(b, 1)])
                ins.then_inc(s["vt_in"], 1)
                for w in range(2):
                    act.wait_ge(s["rem_qk"], b * 2 + (w + 1))
                    nc.scalar.activation(part[:, w, 1, :], qk[:, w, :], ACT.Copy).then_inc(s["cast1"], 1)

            def take_v(b, first):
                act.wait_ge(s["v_done"], b + 1)
                if not first:
                    act.wait_ge(s["pv_done"], b * 4)
                for t in range(HALVES):
                    src = bank[7][:, t * H:(t + 1) * H].rearrange("p (n r d) -> p n r d", r=2, d=HD)
                    ins = nc.scalar.activation(vp[:, t, :, 0:4:3, :], src, ACT.Copy)
                ins.then_inc(s["v_in"], 1)

            def sample(b, par, last):
                if not last:
                    take_qkv(b + 1, False)
                act.wait_ge(s["mt_done"], b + 1)
                nc.scalar.activation(mT[:, :], bank[4][0:NH, 0:S], ACT.Copy).then_inc(s["mT_ready"], 1)
                act.wait_ge(s["mT_ready"], b + 1)
                act.dma_start(qst[96:97, par, :, :], mT[:, :]).then_inc(s["m_row"], 16)
                for n in range(NH):
                    g = n // 4
                    act.wait_ge(s["st_done"], b * NH + (n + 1))
                    if n % 4 == 0 and not (isinstance(b, int) and b == 0 and g < 2):
                        act.wait_ge(s["pv_done"], b * 4 + (g - 1))
                    nc.scalar.activation(ex[:, g % 2, n % 4, :], bank[4 + n % 4][:, :], ACT.Exp, scale=SCALE)\
                        .then_inc(s["exp_done"], 1)
                if not last:
                    take_v(b + 1, False)

            take_qkv(0, True)
            take_v(0, True)
            sample(0, 0, False)
            with act.Fori(0, B // 2 - 1) as i:
                for k in range(2):
                    sample(i * 2 + (k + 1), (k + 1) % 2, False)
            sample(B - 1, 1, True)
            act.wait_ge(s["ld_l1"], 16 * 11)
            act.wait_ge(s["const_pool"], 2)
            act.wait_ge(s["x1_ready"], B)
            nc.scalar.activation(tA[:, :], tA[:, :], ACT.Tanh).then_inc(s["dt_out"], 1)

            def take_projection(b, first):
                act.wait_ge(s["xr_done"], b * 2 + 2)
                if not first:
                    act.wait_ge(s["conv_done"], b)
                for c in range(CT):
                    ins = nc.scalar.activation(xrp[:, c, TAPS - 1:], bank[c // 2][:, (c % 2) * S:(c % 2 + 1) * S],
                                               ACT.Identity, bias=cond[:, c, bass.ds(b, 1)])
                ins.then_inc(s["xr_in"], 1)
                act.wait_ge(s["xr_in"], b + 1)
                for c in range(CT):
                    ins = nc.scalar.activation(acc[:, c, :], xrp[:, c, TAPS - 1:], ACT.Identity,
                                               bias=bcv[:, c:c + 1], scale=wcv[:, c, TAPS - 1:TAPS])
                ins.then_inc(s["tap3_ready"], 1)
                act.wait_ge(s["gate_done"], b * 2 + 2)
                for c2 in range(2):
                    ins = nc.scalar.activation(gateT[:, 2 * c2:2 * c2 + 2, bass.ds(b * S, S)],
                                               bank[2 + c2][:, :].rearrange("p (k s) -> p k s", k=2), ACT.Silu)
                ins.then_inc(s["gate_out"], 1)

            def take_tokens(b):
                for t in range(HALVES):
                    act.wait_ge(s["tok_ready"], b * HALVES + (t + 1))
                    nc.scalar.activation(xc[:, b * HALVES + t, :], bank[5 + t][:, :], ACT.Copy)\
                        .then_inc(s["tok_taken"], 1)

            def gate_conv(b, first):
                act.wait_ge(s["conv_done"], b + 1)
                if not first:
                    act.wait_ge(s["xcT_used"], b)
                nc.scalar.activation(xcT[:, :, :], acc[:, :, :], ACT.Silu).then_inc(s["xcT_ready"], 1)

            take_projection(0, True)
            gate_conv(0, True)
            with act.Fori(1, B) as b:
                take_projection(b, False)
                take_tokens(b - 1)
                gate_conv(b, False)
            take_tokens(B - 1)
            act.wait_ge(s["rt_in"], 3)
            nc.scalar.activation(rt[:, :], var_e[:, :], ACT.Sqrt).then_inc(s["rt_out"], 1)
            act.wait_ge(s["dt_in"], 1)
            nc.scalar.activation(dtt[:, :, :], dtt[:, :, :], ACT.Tanh).then_inc(s["dt_out"], 1)
            act.wait_ge(s["shift_ready"], 1)

            def normalise(b):
                for t in range(HALVES):
                    n = b * HALVES + t
                    nc.scalar.activation(xz[:, t, :], xc[:, n, :], ACT.Identity, bias=shift[:, bass.ds(n, 1)],
                                         scale=rs[:, bass.ds(n, 1)]).then_inc(s["xz_ready"], 1)

            def parts(b, first, last):
                for t in range(HALVES):
                    act.wait_ge(s["xn_ready"], b * HALVES + (t + 1))
                    if not first:
                        act.wait_ge(s["xs_out"], b * (16 * HALVES))
                    nc.scalar.activation(xpart[:, t, 0, :], xn[:, t, :], ACT.Copy).then_inc(s["part0"], 1)
                    nc.scalar.activation(bank[6 + t][:, :], xn[:, t, :], ACT.Square, accum_out=ss[:, bass.ds(b * HALVES + t, 1)])\
                        .then_inc(s["sq_done"], 1)
                if not last:
                    normalise(b + 1)
                for t in range(HALVES):
                    act.wait_ge(s["rem0"], b * HALVES + (t + 1))
                    nc.scalar.activation(xpart[:, t, 1, :], xrem[:, t, :], ACT.Copy).then_inc(s["part1"], 1)

            normalise(0)
            parts(0, True, False)
            with act.Fori(1, B - 1) as b:
                parts(b, False, False)
            parts(B - 1, False, True)
            act.wait_ge(s["sq_done"], NT)
            nc.scalar.activation(nrm[:, :], ss[:, :], ACT.Sqrt).then_inc(s["nrm_ready"], 1)
            with act.Fori(0, NCH // 2) as i:
                for par in range(2):
                    act.wait_ge(s[f"yst{par}"], i * 64)
                    for g in range(CH // 4):
                        n = par * (CH // 4) + g
                        act.wait_ge(s["y_done"], i * (2 * CH // 4) + (n + 1))
                        nc.scalar.activation(yb[:, par, g, :], bank[4 + n % 2][:, :], ACT.Copy)\
                            .then_inc(s["y_taken"], 1)
            with act.Fori(0, B) as b:
                for t in range(HALVES):
                    act.wait_ge(s["o_done"], b * HALVES + (t + 1))
                    act.wait_ge(s["o_out"], b * (16 * HALVES))
                    nc.scalar.activation(ob[:, t, :], bank[6 + t][:, 0:H], ACT.Copy).then_inc(s["ob_ready"], 1)
                    act.wait_ge(s["ob_ready"], b * HALVES + (t + 1))
                    act.dma_start(out[b, t * P:(t + 1) * P, :], ob[:, t, :]).then_inc(s["o_out"], 16)
            act.wait_ge(s["o_out"], 16 * NT)

        @block.tensor
        def _(pe):
            mm = nc.tensor.matmul
            pe.wait_ge(s["dcsum"], 1)
            for w in range(5):
                for o in range(HT):
                    for k in range(HT):
                        st = cond2[:, (0 if w < 3 else HT) + k, :]
                        col = (w * HT + o) * B
                        ins = mm(bank[0][:, col:col + B], wsq[:, w, k, o * P:(o + 1) * P], st, start=k == 0,
                                 stop=k == HT - 1)
            ins.then_inc(s["dcsum"], 1)
            pe.wait_ge(s["ld_c"], 16 * 2)
            pe.wait_ge(s["dc_done"], 1)
            pe.wait_ge(s["const_pool"], 1)

            def transpose_xn(b, first):
                pe.wait_ge(s["xnb_ready"], b + 1)
                if not first:
                    pe.wait_ge(s["att_ready"], b * 2 - 3)
                for k in range(HT):
                    for t in range(HALVES):
                        ins = nc.tensor.transpose(bank[0][:, k * S + t * P:k * S + (t + 1) * P],
                                                  xnb[:, t, k * P:(k + 1) * P], ident[:, :])
                ins.then_inc(s["tr_done"], 1)

            def channels_of(w, bk, b, done, src=None):
                for o in range(HT):
                    for k in range(HT):
                        ins = mm(bank[bk][:, o * S:(o + 1) * S], w5[:, w, k, o * P:(o + 1) * P],
                                 xnT[:, k, :] if src is None else src(k), start=k == 0, stop=k == HT - 1)
                ins.then_inc(s[done], 1)

            def v_tokens(b):
                for t in range(HALVES):
                    for k in range(HT):
                        ins = mm(bank[7][:, t * H:(t + 1) * H], xnT[:, k, t * P:(t + 1) * P], w5[:, 2, k, :],
                                 start=k == 0, stop=k == HT - 1)
                ins.then_inc(s["v_done"], 1)

            def max_scores(b, par, n, first):
                if n >= 4:
                    pe.wait_ge(s["maxes"], b * NH + (n - 3))
                if n == 3:
                    pe.wait_ge(s["v_in"], b + 1)
                for t in range(HALVES):
                    ins = mm(bank[4 + n % 4][:, t * S:(t + 1) * S], qst[0:96, par, HEADS[n], t * P:(t + 1) * P],
                             kst[0:96, par, HEADS[n], :], start=True, stop=True)
                ins.then_inc(s["smax_done"], 1)

            def scores(b, par, g):
                for n in range(4 * g, 4 * g + 4):
                    if n >= 4:
                        pe.wait_ge(s["exp_done"], b * NH + (n - 3))
                    for t in range(HALVES):
                        ins = mm(bank[4 + n % 4][:, t * S:(t + 1) * S], kst[0:97, par, HEADS[n], t * P:(t + 1) * P],
                                 qst[0:97, par, HEADS[n], :], start=True, stop=True)
                    ins.then_inc(s["st_done"], 1)

            def weigh(b, g):
                o, par = g // 2, g % 2
                pe.wait_ge(s["exp_done"], b * NH + (4 * g + 4))
                for sums in range(2):
                    for t in range(HALVES):
                        for r in range(4):
                            lhs = (half_ones[:, par, :] if sums else
                                   vp[:, t, 4 * o + r, 2 * par:2 * par + 2, :].rearrange("p a d -> p (a d)"))
                            ins = mm(bank[2 * o + sums][32 * r:32 * r + 32, 0:S], lhs,
                                     ex[:, g % 2, r, t * S:(t + 1) * S], start=par == 0 and t == 0,
                                     stop=par == 1 and t == HALVES - 1, skip_group_check=True)
                ins.then_inc(s["pv_done"], 1)

            def project_out(b):
                pe.wait_ge(s["att_ready"], b * 2 + 2)
                pe.wait_ge(s["vt_in"], b + 1)
                for w, bk, src in ((3, 0, lambda k: attT[:, k, :]), (4, 1, lambda k: vT[:, k, bass.ds(b * S, S)])):
                    for o in range(HT):
                        for k in range(HT):
                            ins = mm(bank[bk][:, o * S:(o + 1) * S], w5[:, w, k, o * P:(o + 1) * P], src(k),
                                     start=k == 0, stop=k == HT - 1)
                ins.then_inc(s["wu_done"], 1)

            def sample(b, par, turn, first, last):
                pe.wait_ge(s[f"ld_q{par}"], turn * 48 + 48)
                pe.wait_ge(s[f"ld_k{par}"], turn * 48 + 48)
                if not first:
                    pe.wait_ge(s["exp_done"], b * NH)
                for n in range(4):
                    max_scores(b, par, n, first)
                if not last:
                    transpose_xn(b + 1, first)
                    max_scores(b, par, 4, first)
                    max_scores(b, par, 5, first)
                    pe.wait_ge(s["xnT_ready"], b + 2)
                    channels_of(0, 1, b, "q_done")
                    max_scores(b, par, 6, first)
                    max_scores(b, par, 7, first)
                    max_scores(b, par, 8, first)
                    if not first:
                        pe.wait_ge(s["att_ready"], b * 2)
                    channels_of(1, 2, b, "k_done")
                    max_scores(b, par, 9, first)
                    max_scores(b, par, 10, first)
                    channels_of(2, 3, b, "vt_done")
                    for n in range(11, NH):
                        max_scores(b, par, n, first)
                else:
                    for n in range(4, NH):
                        max_scores(b, par, n, first)
                pe.wait_ge(s["maxes"], b * NH + NH)
                for t in range(HALVES):
                    ins = nc.tensor.transpose(bank[4][0:NH, t * P:(t + 1) * P], mx[:, t, :], ident[:, :])
                ins.then_inc(s["mt_done"], 1)
                if not last:
                    pe.wait_ge(s["q_in"], b + 2)
                if not first:
                    project_out(b - 1)
                pe.wait_ge(s["m_row"], b * 16 + 16)
                scores(b, par, 0)
                scores(b, par, 1)
                if not first:
                    pe.wait_ge(s["x1_ready"], b)
                weigh(b, 0)
                scores(b, par, 2)
                weigh(b, 1)
                scores(b, par, 3)
                if not last:
                    pe.wait_ge(s["k_in"], b + 2)
                    pe.wait_ge(s["vt_in"], b + 2)
                weigh(b, 2)
                weigh(b, 3)
                if not last:
                    v_tokens(b + 1)

            transpose_xn(0, True)
            pe.wait_ge(s["xnT_ready"], 1)
            channels_of(0, 1, 0, "q_done")
            channels_of(1, 2, 0, "k_done")
            channels_of(2, 3, 0, "vt_done")
            v_tokens(0)
            sample(0, 0, 0, True, False)
            with pe.Fori(0, B // 2 - 1) as i:
                for k in range(2):
                    sample(i * 2 + (k + 1), (k + 1) % 2, i + k, False, False)
            sample(B - 1, 1, B // 2 - 1, False, True)
            project_out(B - 1)

            pe.wait_ge(s["ld_l1"], 16 * 11)
            pe.wait_ge(s["x1_ready"], B)
            for c in range(CT):
                ins = mm(bank[7][:, c * NS:(c + 1) * NS], wxd[:, c * P:(c + 1) * P], wdt[:, :], start=True, stop=True)
            ins.then_inc(s["wcomp"], 1)
            pe.wait_ge(s["wgain"], 1)
            for j, (lhs, rhs) in enumerate(((None, wxg), (lnb_rep, wx))):
                for c in range(CT):
                    ins = mm(bank[7][:, 64 + 64 * j:64 + 64 * j + NP3], ones[:, :] if lhs is None else lhs[:, c, :],
                             rhs[:, c, :], start=c == 0, stop=c == CT - 1)
            ins.then_inc(s["pconst"], 1)

            def project_in(b, first):
                for c in range(2 * CT):
                    if c == 0 and not first:
                        pe.wait_ge(s["xr_in"], b)
                    if c == CT and not first:
                        pe.wait_ge(s["gate_out"], b)
                    for k in range(HT):
                        ins = mm(bank[c // 2][:, (c % 2) * S:(c % 2 + 1) * S], win[:, k, c * P:(c + 1) * P],
                                 xres[:, k, bass.ds(b * S, S)], start=k == 0, stop=k == HT - 1)
                    if c % 2:
                        ins.then_inc(s["xr_done"] if c < CT else s["gate_done"], 1)

            def to_tokens(b, first):
                pe.wait_ge(s["xcT_ready"], b + 1)
                if not first:
                    pe.wait_ge(s["tok_taken"], b * HALVES)
                for t in range(HALVES):
                    for c in range(CT):
                        ins = nc.tensor.transpose(bank[5 + t][:, c * P:(c + 1) * P], xcT[:, c, t * P:(t + 1) * P],
                                                  ident[:, :])
                    ins.then_inc(s["tok_ready"], 1)
                if not first:
                    pe.wait_ge(s["raw_ready"], b)
                for t in range(HALVES):
                    for c in range(CT):
                        ins = mm(bank[4][:, t * 64:t * 64 + NP3], xcT[:, c, t * P:(t + 1) * P], wxg[:, c, :],
                                 start=c == 0, stop=c == CT - 1)
                ins.then_inc(s["xcT_used"], 1)

            project_in(0, True)
            project_in(1, False)
            to_tokens(0, True)
            with pe.Fori(2, B) as b:
                project_in(b, False)
                to_tokens(b - 1, False)
            to_tokens(B - 1, False)
            pe.wait_ge(s["eb_ready"], 1)
            for j, src in enumerate((adt, cdt)):
                for t in range(HALVES):
                    ins = nc.tensor.transpose(bank[j][:, t * P:(t + 1) * P],
                                              src[:, t, :, :].rearrange("p b d -> p (b d)"), ident[:, :])
            ins.then_inc(s["eb_tr"], 1)
            pe.wait_ge(s["ipc_ready"], 1)
            for j, src in enumerate((ipc, dr)):
                for t in range(HALVES):
                    ins = nc.tensor.transpose(bank[2 + j][:, t * P:(t + 1) * P], src[:, t * P:(t + 1) * P],
                                              ident[:, :])
            ins.then_inc(s["eb_back"], 1)
            pe.wait_ge(s["bsplit"], 2)
            pe.wait_ge(s["c_ready"], 1)

            def u_steps(par, g, first, z_seen):
                for k in range(4):
                    step = 4 * g + k
                    if not first:
                        pe.wait_ge(s["z_ready"], z_seen + (step - 3))
                    mm(bank[k][:, :], bst[:, par, step, :], xst[:, par, step, :], start=True, stop=True)\
                        .then_inc(s["u_done"], 1)

            def y_steps(par, g, z_seen, y_seen):
                pe.wait_ge(s["z_ready"], z_seen + (4 * g + 4))
                pe.wait_ge(s["y_taken"], y_seen)
                for k in range(4):
                    step = 4 * g + k
                    ins = mm(bank[4 + g % 2][32 * k:32 * k + 32, :], cst[:, par, step, :], zst[:, step % ZR, :],
                             start=True, stop=True)
                ins.then_inc(s["y_done"], 1)

            G = CH // 4
            pe.wait_ge(s["ld_x0"], 16 * len(PAIRS))
            pe.wait_ge(s["ld_b0"], 16)
            u_steps(0, 0, True, 0)
            with pe.Fori(0, NCH // 2 - 1) as i:
                for n in range(2 * G):
                    par, g = n // G, n % G
                    nxt = (n + 1) % (2 * G)
                    if nxt % G == 0:
                        q = nxt // G
                        load = i + (2 if q == 0 else 1)
                        pe.wait_ge(s[f"ld_x{q}"], load * (16 * len(PAIRS)))
                        pe.wait_ge(s[f"ld_b{q}"], load * 16)
                    if nxt == 0:
                        u_steps(0, 0, False, i * (2 * CH) + 2 * CH)
                    else:
                        u_steps(nxt // G, nxt % G, False, i * (2 * CH) + (nxt // G) * CH)
                    if g == 0:
                        pe.wait_ge(s["cst_ready"], i * 2 + (par + 1))
                    y_steps(par, g, i * (2 * CH) + par * CH, i * (2 * G) + max(n - 1, 0))
            last = (NCH // 2 - 1)
            for n in range(2 * G):
                par, g = n // G, n % G
                if n + 1 < 2 * G:
                    if (n + 1) % G == 0:
                        pe.wait_ge(s["ld_x1"], (last + 1) * (16 * len(PAIRS)))
                        pe.wait_ge(s["ld_b1"], (last + 1) * 16)
                    u_steps((n + 1) // G, (n + 1) % G, False, last * 2 * CH + (n + 1) // G * CH)
                if g == 0:
                    pe.wait_ge(s["cst_ready"], last * 2 + par + 1)
                y_steps(par, g, last * 2 * CH + par * CH, last * 2 * G + max(n - 1, 0))
            pe.wait_ge(s["y_taken"], NCH * G)
            with pe.Fori(0, B) as b:
                pe.wait_ge(s["x1s_ready"], b + 1)
                for t in range(HALVES):
                    pe.wait_ge(s["ysum_ready"], b * HALVES + (t + 1))
                    pe.wait_ge(s["yg_ready"], b * HALVES + t)
                    for c in range(CT):
                        ins = nc.tensor.transpose(bank[4][:, c * P:(c + 1) * P], ysum[:, t, c * P:(c + 1) * P],
                                                  ident[:, :])
                    ins.then_inc(s["yt_done"], 1)
                    pe.wait_ge(s["yg_ready"], b * HALVES + (t + 1))
                    pe.wait_ge(s["ob_ready"], b * HALVES)
                    for c in range(CT):
                        mm(bank[6 + t][:, 0:H], yg[:, c, :], wo[:, c, :], start=c == 0, stop=False,
                           skip_group_check=True)
                    for k in range(HT):
                        ins = mm(bank[6 + t][:, k * P:(k + 1) * P], x1s[:, k, t * P:(t + 1) * P], ident[:, :],
                                 start=False, stop=k == HT - 1, skip_group_check=True)
                    ins.then_inc(s["o_done"], 1)

        @block.vector
        def _(dve):
            v = nc.vector
            own = Own(dve, s["vec"])

            def statistics(tiles):
                own.settle()
                for n in range(NT):
                    own.mark(v.bn_stats(bn[:, n, :], tiles[:, n, :]))
                own.settle()
                for n in range(NT):
                    own.mark(v.bn_aggr(mv[:, n, :], bn[:, n, :]))
                own.settle()

            dve.wait_ge(s["ld_w"], 32)
            v.tensor_tensor(wsq[:, :, :, :], w5[:, :, :, :], w5[:, :, :, :], ALU.mult)
            v.tensor_tensor(cond2[:, :, :], cond[:, :, :], cond[:, :, :], ALU.mult).then_inc(s["dcsum"], 1)
            dve.wait_ge(s["dcsum"], 2)
            v.tensor_scalar(dcv[:, :, :, :].rearrange("p w o b -> p (w o b)"), bank[0][:, 0:10 * B], EPS_DM, None,
                            ALU.add).then_inc(s["rt_in"], 1)
            dve.wait_ge(s["rt_out"], 1)

            def rsqrt(y, root, x, tmp):
                own.mark(v.reciprocal(y, root))
                own.settle()
                own.mark(v.tensor_tensor(tmp, y, y, ALU.mult))
                own.settle()
                own.mark(v.tensor_tensor(tmp, tmp, x, ALU.mult))
                own.settle()
                own.mark(v.tensor_scalar(tmp, tmp, -0.5, 1.5, ALU.mult, ALU.add))
                own.settle()
                own.mark(v.tensor_tensor(y, y, tmp, ALU.mult))
                own.settle()

            rsqrt(dc[:, :, :, :], dct[:, :, :, :], dcv[:, :, :, :], dct[:, :, :, :])
            own.mark(v.tensor_tensor(vdc[:, :, :], dc[:, 2, :, :], cond[:, HT:2 * HT, :], ALU.mult))
            own.settle()
            v.memset(tick[:, :], 0.0).then_inc(s["dc_done"], 1)
            dve.wait_ge(s["ld_l0"], 32)
            for n in range(NT):
                own.mark(v.tensor_tensor(xt[:, n, :], xt[:, n, :], s1b[:, n // HALVES, :], ALU.mult))
            statistics(xt)
            v.tensor_scalar(var_e[:, :], mv[:, :, 1], EPS_LN, None, ALU.add).then_inc(s["rt_in"], 1)
            dve.wait_ge(s["rt_in"], 2)
            dve.wait_ge(s["rt_out"], 2)
            rsqrt(rs[:, :], rt[:, :], var_e[:, :], rt[:, :])
            dve.wait_ge(s["ld_x"], 16)
            dve.wait_ge(s["const_pool"], 1)

            def normalise(b, first):
                if not first:
                    dve.wait_ge(s["tr_done"], b)
                for t in range(HALVES):
                    n = b * HALVES + t
                    ins = v.tensor_scalar(xnb[:, t, :], xt[:, n, :], mv[:, n, 0:1], rs[:, bass.ds(n, 1)],
                                          ALU.subtract, ALU.mult)
                ins.then_inc(s["xnb_ready"], 1)

            def add_l0(b):
                dve.wait_ge(s["wu_done"], b + 1)
                for bk, w in ((0, 3), (1, 4)):
                    for o in range(HT):
                        tile = xres[:, o, bass.ds(b * S, S)]
                        ins = v.scalar_tensor_tensor(tile, bank[bk][:, o * S:(o + 1) * S], dc[:, w, o, bass.ds(b, 1)],
                                                     tile, ALU.mult, ALU.add)
                    if bk == 0:
                        own.mark(ins)
                        own.settle()
                ins.then_inc(s["x1_ready"], 1)

            def sample(b, first, last):
                if not last:
                    normalise(b + 1, False)
                if not first:
                    dve.wait_ge(s["mt_done"], b)
                for n in range(NH):
                    dve.wait_ge(s["smax_done"], b * NH + (n + 1))
                    v.tensor_reduce(mx[:, :, HEADS[n]:HEADS[n] + 1],
                                    bank[4 + n % 4][:, :].rearrange("p (t k) -> p t k", t=HALVES), AX.X, ALU.max)\
                        .then_inc(s["maxes"], 1)
                if not first:
                    add_l0(b - 1)
                for o in range(HT):
                    dve.wait_ge(s["pv_done"], b * 4 + (2 * o + 2))
                    own.mark(v.reciprocal(rec[:, o, :], bank[2 * o + 1][:, 0:S]))
                    own.settle()
                    v.scalar_tensor_tensor(attT[:, o, :], bank[2 * o][:, 0:S], vdc[:, o, bass.ds(b, 1)], rec[:, o, :],
                                           ALU.mult, ALU.mult).then_inc(s["att_ready"], 1)

            normalise(0, True)
            sample(0, True, False)
            with dve.Fori(0, B // 2 - 1) as i:
                own.enter(i, 6)
                for k in range(2):
                    sample(i * 2 + (k + 1), False, False)
            own.leave(B // 2 - 1)
            sample(B - 1, False, True)
            add_l0(B - 1)
            dve.wait_ge(s["ld_l1"], 16 * 11)
            dve.wait_ge(s["wcomp"], 1)
            own.mark(v.tensor_copy(wx[:, :, 2 * NS:], bank[7][:, 0:CT * NS].rearrange("p (c n) -> p c n", c=CT)))
            own.settle()
            for c in range(CT):
                v.tensor_scalar(wxg[:, c, :], wx[:, c, :], lnt[:, 0, c:c + 1], None, ALU.mult)
                ins = v.tensor_scalar(lnb_rep[:, c, :], ones[:, :], lnt[:, 1, c:c + 1], None, ALU.mult)
            ins.then_inc(s["wgain"], 1)
            dve.wait_ge(s["pconst"], 1)
            v.tensor_copy(proj_sum[:, :], bank[7][:, 64:64 + NP3])
            own.mark(v.tensor_copy(proj_off[:, :], bank[7][:, 128:128 + NP3]))
            own.settle()
            own.mark(v.tensor_tensor(proj_off[:, 2 * NS:], proj_off[:, 2 * NS:], bdt[:, :], ALU.add))
            own.settle()

            def convolve():
                for k in range(TAPS - 1):
                    for c in range(CT):
                        ins = v.scalar_tensor_tensor(acc[:, c, :], xrp[:, c, k:k + S], wcv[:, c, k:k + 1],
                                                     acc[:, c, :], ALU.mult, ALU.add)
                    if k < TAPS - 2:
                        own.mark(ins)
                        own.settle()
                ins.then_inc(s["conv_done"], 1)

            def take_raw(b):
                dve.wait_ge(s["tok_taken"], b * HALVES + HALVES)
                dve.wait_ge(s["xcT_used"], b + 1)
                v.tensor_copy(raw[:, bass.ds(b * HALVES, HALVES), :],
                              bank[4][:, 0:2 * 64].rearrange("p (t n) -> p t n", t=HALVES)[:, :, 0:NP3])\
                    .then_inc(s["raw_ready"], 1)
                for t in range(HALVES):
                    ins = v.bn_stats(bn[:, b * HALVES + t, :], xc[:, b * HALVES + t, :])
                own.mark(ins)

            dve.wait_ge(s["tap3_ready"], 1)
            convolve()
            with dve.Fori(1, B) as b:
                own.enter(b - 1, TAPS - 1)
                dve.wait_ge(s["tap3_ready"], b + 1)
                convolve()
                take_raw(b - 1)
            own.leave(B - 1)
            take_raw(B - 1)
            own.settle()
            for n in range(NT):
                own.mark(v.bn_aggr(mv[:, n, :], bn[:, n, :]))
            own.settle()
            v.tensor_scalar(var_e[:, :], mv[:, :, 1], EPS_LN, None, ALU.add).then_inc(s["rt_in"], 1)
            dve.wait_ge(s["rt_in"], 3)
            dve.wait_ge(s["rt_out"], 3)
            rsqrt(rs[:, :], rt[:, :], var_e[:, :], rt[:, :])
            def wide(ap):
                return ap.unsqueeze(2).broadcast_to([P, NT, NP3])

            def rows(ap):
                return ap.unsqueeze(1).broadcast_to([P, NT, ap.shape[1]])

            own.mark(v.tensor_tensor(raw[:, :, :], raw[:, :, :], wide(rs[:, :]), ALU.mult))
            own.mark(v.tensor_tensor(var_e[:, :], mv[:, :, 0], rs[:, :], ALU.mult))
            own.settle()
            v.tensor_scalar(shift[:, :], var_e[:, :], -1.0, None, ALU.mult).then_inc(s["shift_ready"], 1)
            own.mark(v.tensor_tensor(t48[:, :, :], wide(var_e[:, :]), rows(proj_sum[:, :]), ALU.mult))
            own.settle()
            own.mark(v.tensor_tensor(raw[:, :, :], raw[:, :, :], t48[:, :, :], ALU.subtract))
            own.settle()
            own.mark(v.tensor_tensor(raw[:, :, :], raw[:, :, :], rows(proj_off[:, :]), ALU.add))
            own.settle()
            v.tensor_copy(dtt[:, :, :], raw[:, :, 2 * NS:]).then_inc(s["dt_in"], 1)
            own.mark(v.tensor_copy(cdt[:, :, :, :].rearrange("p t b d -> p b t d"),
                                   raw[:, :, NS:2 * NS].rearrange("p (b t) d -> p b t d", t=HALVES)))
            own.mark(v.tensor_reduce(ybias[:, :].unsqueeze(2), raw[:, :, NS:2 * NS], AX.X, ALU.add))
            own.settle()
            own.mark(v.tensor_scalar(ybias[:, :], ybias[:, :], -BOUND, None, ALU.mult))
            dve.wait_ge(s["dt_out"], 2)
            own.mark(v.tensor_tensor(dtt[:, :, :], dtt[:, :, :], rows(tA[:, :]), ALU.mult))
            own.settle()
            v.tensor_scalar(adt[:, :, :, :].rearrange("p t b d -> p b t d"),
                            dtt[:, :, :].rearrange("p (b t) d -> p b t d", t=HALVES), -STEP, 1.0, ALU.mult, ALU.add)\
                .then_inc(s["eb_ready"], 1)
            dve.wait_ge(s["eb_tr"], 1)
            own.mark(v.tensor_tensor_scan(pcum[:, :], bank[0][:, 0:S], one_row[:, :], 1.0, ALU.mult, ALU.mult))
            own.settle()
            own.mark(v.reciprocal(ipc[:, :], pcum[:, :]))
            own.mark(v.tensor_tensor(cP[:, :], bank[1][:, 0:S], pcum[:, :], ALU.mult))
            own.settle()
            own.mark(v.tensor_scalar(rr[:, 1:], ipc[:, :], BOUND, None, ALU.mult))
            own.mark(v.tensor_scalar(hi[:, :], ipc[:, :], 2 * BOUND, None, ALU.mult))
            own.settle()
            v.tensor_tensor(dr[:, :], rr[:, 1:], rr[:, 0:S], ALU.subtract).then_inc(s["ipc_ready"], 1)
            v.memset(tick[:, :], 0.0).then_inc(s["c_ready"], 1)
            dve.wait_ge(s["eb_back"], 1)

            def split(parts, rem):
                flat = [parts[:, k, :, :].rearrange("p t n -> p (t n)") for k in range(3)]
                r = rem[:, :, :].rearrange("p t n -> p (t n)")
                for k in range(2):
                    own.mark(v.tensor_copy(flat[k], r))
                    own.settle()
                    own.mark(v.tensor_tensor(r, r, flat[k], ALU.subtract))
                    own.settle()
                v.tensor_copy(flat[2], r).then_inc(s["bsplit"], 1)

            own.mark(v.tensor_copy(drem[:, :, :].rearrange("p t n -> p (t n)"), bank[3][:, 0:S]))
            own.settle()
            split(dpart, drem)
            def finish_rows(b, first):
                for t in range(HALVES):
                    dve.wait_ge(s["xz_ready"], b * HALVES + (t + 1))
                    if not first:
                        dve.wait_ge(s["rem0"], b * HALVES + (t - 1))
                        dve.wait_ge(s["sq_done"], b * HALVES + (t - 1))
                        dve.wait_ge(s["dx_ready"], b * HALVES + (t - 1))
                    own.mark(v.tensor_tensor(xn[:, t, :], xz[:, t, :], lnr[:, 0, :], ALU.mult))
                for t in range(HALVES):
                    own.settle(HALVES - 1 - t)
                    v.tensor_tensor(xn[:, t, :], xn[:, t, :], lnr[:, 1, :], ALU.add).then_inc(s["xn_ready"], 1)
                for t in range(HALVES):
                    dve.wait_ge(s["part0"], b * HALVES + (t + 1))
                    if not first:
                        dve.wait_ge(s["parts_ready"], b * HALVES + (t - 1))
                    v.tensor_tensor(xrem[:, t, :], xn[:, t, :], xpart[:, t, 0, :], ALU.subtract)\
                        .then_inc(s["rem0"], 1)

            finish_rows(0, True)
            with dve.Fori(1, B) as b:
                own.enter(b - 1, HALVES)
                finish_rows(b, False)
            own.leave(B - 1)
            dve.wait_ge(s["nrm_ready"], 1)
            own.mark(v.tensor_scalar(nrm[:, :], nrm[:, :], 1.0, None, ALU.min))
            own.settle()
            own.mark(v.tensor_tensor(bnt[:, :, :, :].rearrange("p t b d -> p b t d"),
                                     raw[:, :, 0:NS].rearrange("p (b t) d -> p b t d", t=HALVES),
                                     nrm[:, :].rearrange("p (b t) -> p b t", t=HALVES).unsqueeze(3)
                                     .broadcast_to([P, B, HALVES, NS]), ALU.mult))
            own.settle()
            own.mark(v.tensor_tensor(brem[:, :, :].rearrange("p t n -> p (t n)"), bank[2][:, 0:S],
                                     bnt[:, :, :, :].rearrange("p t b d -> p (t b d)"), ALU.mult))
            own.settle()
            split(bpart, brem)
            for t in range(S):
                dve.wait_ge(s["u_done"], t + 1)
                if t > 0:
                    dve.wait_ge(s["z_ready"], t)
                if t % 4 == 0 and t >= ZR:
                    dve.wait_ge(s["y_done"], (t - ZR) // 4 + 1)
                v._custom_dve(bass.dve_ops.TENSOR_ADD_SAT, out=zst[:, t % ZR, :], in0=zst[:, (t - 1) % ZR, :],
                              in1=bank[t % 4][:, :], s0=hi[:, t:t + 1], s1=0.0).then_inc(s["z_ready"], 1)
            with dve.Fori(0, B) as b:
                for t in range(HALVES):
                    n = b * HALVES + t
                    dve.wait_ge(s[f"ld_y{t}"], b * 16 + 16)
                    dve.wait_ge(s["yt_done"], b * HALVES)
                    v.scalar_tensor_tensor(ysum[:, t, :], ytk[:, t, :], ybias[:, bass.ds(n, 1)], xc[:, n, :],
                                           ALU.add, ALU.add).then_inc(s["ysum_ready"], 1)
                    dve.wait_ge(s["yt_done"], b * HALVES + (t + 1))
                    dve.wait_ge(s["o_done"], b * HALVES + t)
                    v.tensor_tensor(yg[:, :, :], bank[4][:, :].rearrange("p (c s) -> p c s", c=CT),
                                    gateT[:, :, bass.ds(b * S + t * P, P)], ALU.mult).then_inc(s["yg_ready"], 1)


def kernel(x, cond_2048, L0_cond_q_weight, L0_cond_k_weight, L0_cond_v_weight, L0_cond_w_weight, L0_cond_u_weight,
           L1_cond_W_in, L1_cond_W_conv, L1_cond_b_conv, L1_cond_ln_g, L1_cond_ln_b, L1_cond_W_xproj, L1_cond_W_dt,
           L1_cond_b_dt, L1_cond_A_log, L1_cond_D, L1_cond_W_out):
    import concourse.bacc as bacc
    from concourse.bass_utils import run_bass_kernel_spmd

    def channels(a, width):
        return np.asarray(a).reshape(-1, P, width).transpose(1, 0, 2)

    x, cond = np.asarray(x), np.asarray(cond_2048)
    w5 = np.stack([channels(np.asarray(w).T, H) for w in (L0_cond_q_weight, L0_cond_k_weight, L0_cond_v_weight,
                                                          L0_cond_w_weight, L0_cond_u_weight)], axis=1)
    per_channel = [np.asarray(a).reshape(CT, P).T for a in (L1_cond_ln_g, L1_cond_ln_b)]
    p = np.arange(P)
    arrays = {
        "x_tok": x.reshape(NT, P, H).transpose(1, 0, 2),
        "xT": channels(x.reshape(B * S, H).T, B * S),
        "s1_row": cond[:, :H],
        "condT": channels(cond.T, B),
        "w5T": w5,
        "winT": channels(np.asarray(L1_cond_W_in).T, 2 * C),
        "wconv": np.asarray(L1_cond_W_conv).reshape(CT, P, TAPS).transpose(1, 0, 2),
        "bconv": np.asarray(L1_cond_b_conv).reshape(CT, P).T,
        "ln_row": np.stack([np.asarray(a) for a in (L1_cond_ln_g, L1_cond_ln_b, L1_cond_D)]),
        "lnT": np.stack(per_channel, axis=1),
        "wxT": channels(np.asarray(L1_cond_W_xproj).T, NP3),
        "wxdt": np.asarray(L1_cond_W_xproj)[2 * NS:],
        "wdtT": np.asarray(L1_cond_W_dt).T,
        "bdt_row": np.asarray(L1_cond_b_dt),
        "alog_row": np.asarray(L1_cond_A_log),
        "woT": channels(np.asarray(L1_cond_W_out).T, H),
        "ident_d": np.eye(P, dtype=np.float32),
        "mask8_d": (p[:, None] // NS == np.arange(B)).astype(np.float32),
    }
    arrays = {k: np.ascontiguousarray(a) for k, a in arrays.items()}
    nc = bacc.Bacc("TRN2", target_bir_lowering=False, num_devices=1)
    aps = {k: nc.dram_tensor(k, a.shape, mybir.dt.from_np(a.dtype), kind="ExternalInput").ap()
           for k, a in arrays.items()}
    out = nc.dram_tensor("out", (B, S, H), F32, kind="ExternalOutput").ap()
    build(nc, *aps.values(), out)
    r = run_bass_kernel_spmd(nc, [arrays], core_ids=[0])
    return r.results[0]["out"]
```

```python
from contextlib import ExitStack

import numpy as np

import concourse.bass as bass
from concourse import mybir

F32 = mybir.dt.float32
BF16 = mybir.dt.bfloat16
ALU = mybir.AluOpType
ACT = mybir.ActivationFunctionType
AX = mybir.AxisListType

P = 128
B, S, H = 8, 256, 256
NH, HD = 16, 16
C, NS = 512, 16
TAPS = 4
HALVES = S // P
NT = B * HALVES
HT, CT = H // P, C // P
BOUND = 10.0
STEP = 0.01
SCALE = float(HD) ** -0.5
EPS_LN, EPS_DM = 1e-5, 1e-8
NP3 = 3 * NS
PAIRS = [(0, 0), (1, 0), (2, 0), (0, 1), (1, 1), (0, 2)]
KX = len(PAIRS) * B
KU = KX + 3
XS = 4
CH = 8
NCH = S // CH
ROUNDS = NCH // 2
FIRST_TILE = ROUNDS // 2 + 1
IN_SCAN = ROUNDS - FIRST_TILE
TAIL = [(n % B, n // B) for n in range(IN_SCAN, NT)]
HEADS = [2 * (2 * r + par) + o for o in range(HT) for par in range(2) for r in range(4)]
EARLY = 4
BD_J = B * (S * P)


class Own:

    def __init__(self, eng, sem):
        self.eng, self.sem, self.base, self.n, self.start = eng, sem, 0, 0, 0

    def enter(self, i, per):
        self.start += self.n
        self.n, self.per = 0, per
        self.base = i * per + self.start

    def leave(self, trips):
        assert self.n == self.per, (self.n, self.per)
        self.start += trips * self.per
        self.base, self.n = self.start, 0

    def mark(self, ins):
        ins.then_inc(self.sem, 1)
        self.n += 1

    def settle(self, back=0):
        self.eng.wait_ge(self.sem, self.base + self.n - back)


def build(nc, x_tok, xT, s1_row, condT, w5T, winT, wconv, bconv, ln_row, lnT, wxT, wxdt, wdtT, bdt_row, alog_row,
          woT, ident_d, mask8_d, out):
    with ExitStack() as ctx:
        def sb(name, shape, dt=F32):
            return ctx.enter_context(nc.sbuf_tensor(name, shape, dt))

        def sem(name):
            return ctx.enter_context(nc.semaphore(name))

        xs_d = nc.dram_tensor("xs_d", (3, B, S, C), BF16, kind="Internal").ap()
        bd_d = nc.dram_tensor("bd_d", (KU * S * P + 2 * B * NS,), BF16, kind="Internal").ap()
        qk_d = nc.dram_tensor("qk_d", (2, 2, 3, HD, NH, S), BF16, kind="Internal").ap()
        y_d = nc.dram_tensor("y_d", (S, B, C), F32, kind="Internal").ap()

        bank = [ctx.enter_context(nc.psum_tensor(f"bank{i}", [P, 512], F32)) for i in range(8)]

        ident = sb("ident", [P, P])
        mask8 = sb("mask8", [P, 32])
        ones = sb("ones", [P, P])
        cond = sb("cond", [P, CT, B])
        win = sb("win", [P, HT, 2 * C])
        wcv = sb("wcv", [P, CT, TAPS])
        bcv = sb("bcv", [P, CT])
        lnt = sb("lnt", [P, 2, CT])
        lnr = sb("lnr", [P, 3, C])
        wx = sb("wx", [P, CT, NP3])
        wxg = sb("wxg", [P, CT, NP3])
        wxd = sb("wxd", [NS, C])
        wdt = sb("wdt", [NS, NS])
        bdt = sb("bdt", [P, NS])
        tA = sb("tA", [P, NS])
        wo = sb("wo", [P, CT, H])
        lnb_rep = sb("lnb_rep", [P, CT, P])
        proj_mean = sb("proj_mean", [P, NP3])
        proj_off = sb("proj_off", [P, NP3])
        cond2 = sb("cond2", [P, CT, B])
        dc = sb("dc", [P, 5, HT, B])
        dcv = sb("dcv", [P, 5, HT, B])
        dct = sb("dct", [P, 5, HT, B])
        vdc = sb("vdc", [P, HT, B])
        half_ones = sb("half_ones", [P, 2, 2 * HD])

        xres = sb("xres", [P, HT, B * S])
        raw = sb("raw", [P, NT, NP3])
        mv = sb("mv", [P, NT, 2])
        bn = sb("bn", [P, NT, 6])
        tick = sb("tick", [P, 1])
        var_e = sb("var_e", [P, NT])
        rt = sb("rt", [P, NT])
        rs = sb("rs", [P, NT])
        ybias = sb("ybias", [P, S // 4])

        hi = sb("hi", [P, S])
        cP = sb("cP", [P, S])
        l0 = ExitStack()

        def sb0(name, shape, dt=F32):
            return l0.enter_context(nc.sbuf_tensor(name, shape, dt))

        w5 = sb0("w5", [P, 5, HT, H])
        xt = sb0("xt", [P, NT, H])
        s1b = sb0("s1b", [P, B, H])
        wsq = sb0("wsq", [P, 5, HT, H])
        xnb = sb0("xnb", [P, HALVES, H])
        xnT = sb0("xnT", [P, HT, S])
        qk = sb0("qk", [P, 2, HT * S])
        part = sb0("part", [P, 2, 3, HT * S], BF16)
        qst = sb0("qst", [P, 2, NH, S], BF16)
        kst = sb0("kst", [P, 2, NH, S], BF16)
        vT = sb0("vT", [P, HT, B * S])
        vp = sb0("vp", [P, 2, HALVES, NH // 2, 4, HD])
        mx = sb0("mx", [P, HALVES, NH])
        mT = sb0("mT", [NH, S], BF16)
        ex = sb0("ex", [P, 2, 4, 512])
        esum = sb0("esum", [P, 2, 4, S])
        rec = sb0("rec", [P, HT, S])
        attT = sb0("attT", [P, HT, S])
        l0.close()
        ZR = 8
        zst = sb("zst", [P, ZR, C])
        cst = sb("cst", [P, 2, CH, 32])
        xst = sb("xst", [P, 2, CH, C], BF16)
        bst = sb("bst", [P, 2, CH, P], BF16)
        yb = sb("yb", [P, 2, CH // 4, C])
        gateT = sb("gateT", [P, CT, B * S])
        xc = sb("xc", [P, NT, C])
        l1 = ExitStack()

        def sb1(name, shape, dt=F32):
            return l1.enter_context(nc.sbuf_tensor(name, shape, dt))

        ss = sb1("ss", [P, NT])
        nrm = sb1("nrm", [P, NT])
        adt = sb1("adt", [P, HALVES, B, NS])
        cdt = sb1("cdt", [P, HALVES, B, NS])
        bnt = sb1("bnt", [P, HALVES, B, NS])
        dtt = sb1("dtt", [P, NT, NS])
        ct10 = dtt[:, :, :].rearrange("p n d -> p (n d)")
        pcum = sb1("pcum", [P, S])
        one_row = sb1("one_row", [P, S])
        ipc = sb1("ipc", [P, S])
        rr = sb1("rr", [P, S + 1])
        dr = sb1("dr", [P, S])
        bpart = sb1("bpart", [P, 3, HALVES, B * NS], BF16)
        dpart = sb1("dpart", [P, 3, HALVES, B * NS], BF16)
        rem = sb1("rem", [P, HALVES, B * NS])
        zeros = sb1("zeros", [P, 2048], BF16)
        conv_bufs = ExitStack()

        def sbc(name, shape, dt=F32):
            return conv_bufs.enter_context(nc.sbuf_tensor(name, shape, dt))

        xrp = sbc("xrp", [P, CT, TAPS - 1 + S])
        acc = sbc("acc", [P, CT, S])
        xcT = sbc("xcT", [P, CT, S])
        conv_bufs.close()
        xpart = sb1("xpart", [P, HALVES * XS, 3, C], BF16)
        xrem = sb1("xrem", [P, 2, C])
        l1.close()
        ytk = sb("ytk", [P, 4, C])
        ysum = sb("ysum", [P, 2, C])
        yT = sb("yT", [P, CT, P])
        yg = sb("yg", [P, 2, CT, P])
        x1s = sb("x1s", [P, HT, P])
        ob = sb("ob", [P, 2, H])

        names = """ld_first ld_rest ld_w ld_x ld_l1 ld_c zfill vec_own pool_own const_pool wsq_ready dcsum dc_done rt_in
            rt_out xnb_ready tr_done xnT_ready q_done k_done vt_done v_done q_in k_in vt_in v_in cast0 rem_qk
            cast1 part_ready pw ld_q0 ld_q1 ld_k0 ld_k1 m_row smax_done maxes mt_done mT_ready st_done exp_done
            es_ready pv_done att_ready wu_done x1_ready wcomp wgain pconst xr_done xr_in tap3_ready gate_done
            gate_out conv_done xcT_ready xcT_used raw_ready tok_ready tok_taken xn_ready sq_done part0 part1 rem0
            parts_ready xs_out0 xs_out1 xs_out2 xs_out3 dx_ready nrm_ready dt_in dt_out eb_ready eb_tr ipc_ready eb_back
            bsplit
            bd_out0 bd_out1 c_ready ld_x0 ld_b0 ld_x1 ld_b1 u_done z_ready y_done y_taken yst0 yst1 cst_ready
            ld_y0 ld_y1 ld_y2 ld_y3 ld_tile ysum_ready yt_done yg_ready yt_taken o_done ob_ready o_out0 o_out1
            x1s_ready ct_ready yb_done ybias_ready tsum_ready tt_done tg_ready to_done tb_ready
           """.split()
        s = {n: sem(n) for n in names}

        block = ctx.enter_context(nc.Block())

        @block.sync
        def _(sp):
            for dst, src in ((xt[:, 0:HALVES, :], x_tok[:, 0:HALVES, :]),
                             (s1b[:, :, :], s1_row.partition_broadcast(P))):
                sp.dma_start(dst, src).then_inc(s["ld_first"], 16)
            for dst, src in ((ident[:, :], ident_d), (mask8[:, :], mask8_d)):
                sp.dma_start(dst, src).then_inc(s["ld_c"], 16)
            for dst, src in ((cond[:, :, :], condT), (w5[:, :, :, :], w5T)):
                sp.dma_start(dst, src).then_inc(s["ld_w"], 16)
            sp.dma_start(xt[:, HALVES:, :], x_tok[:, HALVES:, :]).then_inc(s["ld_rest"], 16)
            sp.dma_start(xres[:, :, :], xT).then_inc(s["ld_x"], 16)
            for dst, src in ((win[:, :, :], winT), (wcv[:, :, :], wconv), (bcv[:, :], bconv), (lnt[:, :, :], lnT),
                             (lnr[:, :, :], ln_row.partition_broadcast(P)), (wx[:, :, :], wxT), (wxd[:, :], wxdt),
                             (wdt[:, :], wdtT), (bdt[:, :], bdt_row.partition_broadcast(P)),
                             (tA[:, :], alog_row.partition_broadcast(P)), (wo[:, :, :], woT)):
                sp.dma_start(dst, src).then_inc(s["ld_l1"], 16)

            def stack(b, par, turn, first):
                sp.wait_ge(s["part_ready"], b * 2 + 2)
                if not first:
                    sp.wait_ge(s[f"ld_q{par}"], turn * 48)
                    sp.wait_ge(s[f"ld_k{par}"], turn * 48)
                for hh in range(NH // HT):
                    sp.dma_start(qk_d[par, :, :, :, hh * HT:(hh + 1) * HT, :].rearrange("w k d h s -> d (w k) (h s)"),
                                 part[hh * HD:(hh + 1) * HD, :, :, :].rearrange("p w k s -> p (w k) s"))\
                      .then_inc(s["pw"], 16)
                sp.wait_ge(s["pw"], b * (16 * NH // HT) + 16 * NH // HT)
                for w, name, st in ((0, "q", qst), (1, "k", kst)):
                    if not first:
                        sp.wait_ge(s["st_done"], b * NH - NH)
                    at = 0
                    for run in (3, 2, 1):
                        src = qk_d[par, w, 0:run] if w == 0 else qk_d[par, w, 3 - run:3]
                        sp.dma_start(st[at:at + run * HD, par, :, :], src.rearrange("k d h s -> (k d) h s"))\
                          .then_inc(s[f"ld_{name}{par}"], 16)
                        at += run * HD

            stack(0, 0, 0, True)
            stack(1, 1, 0, True)
            with sp.Fori(0, B // 2 - 1) as i:
                for k in range(2):
                    stack(i * 2 + (k + 2), k, i + 1, False)

            def store_parts(i, slots):
                for k in slots:
                    b = i * XS + k
                    for t in range(HALVES):
                        sp.wait_ge(s["parts_ready"], b * HALVES + (t + 1))
                        sp.dma_start(xs_d[:, b, t * P:(t + 1) * P, :].rearrange("k p c -> p k c"),
                                     xpart[:, HALVES * k + t, :, :]).then_inc(s[f"xs_out{k}"], 16)

            store_parts(0, range(XS))
            store_parts(1, range(XS - 2))
            sp.wait_ge(s["bsplit"], 1)
            sp.wait_ge(s["zfill"], 16)
            for k in range(3):
                row = bd_d[(KX + k) * S * P:(KX + k + 1) * S * P].rearrange("(t c) -> t c", c=P)
                for t in range(HALVES):
                    sp.dma_start(row[t * P:(t + 1) * P], dpart[:, k, t, :]).then_inc(s[f"bd_out{t}"], 16)
            store_parts(1, range(XS - 2, XS))
            bd_v = bd_d[0:KU * S * P].rearrange("(k t c) -> k t c", t=S, c=P)

            def load_x(par, ch):
                at = 0
                for run in (3, 2, 1):
                    sp.dma_start(xst[at:at + run * B, par, :, :],
                                 xs_d[0:run, :, bass.ds(ch * CH, CH), :].rearrange("k b t c -> (k b) t c"))\
                      .then_inc(s[f"ld_x{par}"], 16)
                    at += run * B

            def load_b(par, ch):
                sp.dma_start(bst[0:KU, par, :, :], bd_v[:, bass.ds(ch * CH, CH), :]).then_inc(s[f"ld_b{par}"], 16)

            def store_b(t):
                for j, (_, bp) in enumerate(PAIRS):
                    rows = bd_d[j * BD_J:j * BD_J + B * (S * P + NS)].rearrange("(b q) -> b q", b=B)[:, 0:S * P]
                    rows = rows.rearrange("b (t c) -> t b c", c=P)[:, :, 0:NS]
                    sp.dma_start(rows[t * P:(t + 1) * P], bpart[:, bp, t, :].rearrange("p (b d) -> p b d", b=B))\
                      .then_inc(s[f"bd_out{t}"], 16)

            def store_chunk(par, ch):
                for k in range(4):
                    sp.dma_start(y_d[bass.ds(ch * CH, CH), :, :].rearrange("(g k) b c -> k b g c", k=4)[k],
                                 yb[32 * k:32 * k + B, par, :, :]).then_inc(s[f"yst{par}"], 16)

            sp.wait_ge(s["bsplit"], 2)
            store_b(0)
            sp.wait_ge(s["const_pool"], 3)
            for k in range(XS):
                sp.wait_ge(s[f"xs_out{k}"], 16 * NT // XS)
            load_x(0, 0)
            load_x(1, 1)
            sp.wait_ge(s["bd_out0"], 16 * (len(PAIRS) + 3))
            load_b(0, 0)
            load_b(1, 1)
            store_b(1)
            sp.wait_ge(s["bd_out1"], 16 * (len(PAIRS) + 3))

            def round_of(i, tile):
                if tile is not None:
                    if not (isinstance(tile, int) and tile == 0):
                        sp.wait_ge(s["ysum_ready"], tile)
                    sp.dma_start(ytk[:, 0, :], y_d[0:P, tile, :]).then_inc(s["ld_tile"], 16)
                for par in range(2):
                    sp.wait_ge(s["u_done"], i * (2 * CH) + (par + 1) * CH)
                    load_x(par, i * 2 + (par + 2))
                    load_b(par, i * 2 + (par + 2))
                for par in range(2):
                    sp.wait_ge(s["y_taken"], i * (2 * CH // 4) + (par + 1) * (CH // 4))
                    store_chunk(par, i * 2 + par)

            with sp.Fori(0, FIRST_TILE - 1) as i:
                round_of(i, None)
            for par in range(2):
                sp.wait_ge(s[f"yst{par}"], (FIRST_TILE - 1) * 64)
            round_of(FIRST_TILE - 1, 0)
            with sp.Fori(FIRST_TILE, ROUNDS - 1) as i:
                round_of(i, i - (FIRST_TILE - 1))
            b, half = TAIL[0]
            sp.wait_ge(s["ysum_ready"], IN_SCAN)
            sp.dma_start(ytk[:, 0, :], y_d[half * P:(half + 1) * P, b, :]).then_inc(s["ld_y0"], 16)
            for par in range(2):
                sp.wait_ge(s["y_taken"], (ROUNDS - 1) * (2 * CH // 4) + (par + 1) * (CH // 4))
                store_chunk(par, NCH - 2 + par)
            for par in range(2):
                sp.wait_ge(s[f"yst{par}"], ROUNDS * 64)
            for n in range(1, len(TAIL)):
                b, half = TAIL[n]
                if n >= 4:
                    sp.wait_ge(s["tsum_ready"], n - 3)
                sp.dma_start(ytk[:, n % 4, :], y_d[half * P:(half + 1) * P, b, :]).then_inc(s[f"ld_y{n % 4}"], 16)

        @block.gpsimd
        def _(pool):
            own = Own(pool, s["pool_own"])
            own.mark(nc.gpsimd.memset(kst[96:P, :, :, :], -1.0))
            own.settle()
            nc.gpsimd.memset(vp[:, :, :, :, :, :], 0.0)
            nc.gpsimd.memset(half_ones[:, :, :], 0.0)
            own.mark(nc.gpsimd.memset(ones[:, :], 1.0))
            own.settle()
            nc.gpsimd.memset(half_ones[:, 0, 0:HD], 1.0)
            nc.gpsimd.memset(half_ones[:, 1, HD:2 * HD], 1.0).then_inc(s["const_pool"], 1)
            with pool.Fori(0, B) as b:
                for w in range(2):
                    pool.wait_ge(s["cast0"], b * 2 + (w + 1))
                    nc.gpsimd.tensor_tensor(qk[:, w, :], qk[:, w, :], part[:, w, 2 * w, :], ALU.subtract)\
                        .then_inc(s["rem_qk"], 1)
                for w in range(2):
                    pool.wait_ge(s["cast1"], b * 2 + (w + 1))
                    nc.gpsimd.tensor_tensor(part[:, w, 2 - 2 * w, :], qk[:, w, :], part[:, w, 1, :], ALU.subtract)\
                        .then_inc(s["part_ready"], 1)
            pool.wait_ge(s["x1_ready"], B)
            nc.gpsimd.memset(xrp[:, :, 0:TAPS - 1], 0.0).then_inc(s["const_pool"], 1)
            nc.gpsimd.memset(xst[:, :, :, :], 1.0)
            nc.gpsimd.memset(bst[:, :, :, :], 0.0)
            nc.gpsimd.memset(cst[:, :, :, :], 0.0)
            nc.gpsimd.memset(rr[:, 0:1], BOUND)
            nc.gpsimd.memset(zst[:, ZR - 1, :], BOUND)
            own.mark(nc.gpsimd.memset(zeros[:, :], 0.0))
            own.settle()
            nc.gpsimd.memset(one_row[:, :], 1.0).then_inc(s["const_pool"], 1)
            pool.dma_start(bd_d[0:KX * S * P].rearrange("(p r z) -> p r z", p=P, z=2048),
                           zeros[:, :].unsqueeze(1).broadcast_to([P, KX * S * P // (P * 2048), 2048]))\
                .then_inc(s["zfill"], 16)
            with pool.Fori(0, B // XS) as i:
                for k in range(XS):
                    b = i * XS + k
                    for t in range(HALVES):
                        buf = HALVES * k + t
                        pool.wait_ge(s["part1"], b * HALVES + (t + 1))
                        nc.gpsimd.tensor_tensor(xpart[:, buf, 2, :], xrem[:, t, :], xpart[:, buf, 1, :],
                                                ALU.subtract).then_inc(s["parts_ready"], 1)
            pool.wait_ge(s["c_ready"], 1)

            def fill_chunk(par, ch):
                nc.gpsimd.tensor_tensor(cst[:, par, :, 0:B],
                                        cP[:, bass.ds(ch * CH, CH)].unsqueeze(2).broadcast_to([P, CH, B]),
                                        mask8[:, 0:B].unsqueeze(1).broadcast_to([P, CH, B]), ALU.mult)\
                    .then_inc(s["cst_ready"], 1)

            fill_chunk(0, 0)
            fill_chunk(1, 1)

            def round_of(i, tile, last):
                if tile is not None:
                    first = isinstance(tile, int) and tile == 0
                    pool.wait_ge(s["ld_tile"], tile * 16 + 16)
                    if not first:
                        pool.wait_ge(s["yt_done"], tile)
                    nc.gpsimd.tensor_tensor(ysum[:, 0, :], ytk[:, 0, :], xc[:, tile * HALVES, :], ALU.add)\
                        .then_inc(s["ysum_ready"], 1)
                    if not first:
                        pool.wait_ge(s["o_done"], tile)
                    nc.gpsimd.tensor_copy(x1s[:, :, :], xres[:, :, bass.ds(tile * S, P)]).then_inc(s["x1s_ready"], 1)
                    pool.wait_ge(s["yt_taken"], tile + 1)
                    nc.gpsimd.tensor_tensor(yg[:, 0, :, :], yT[:, :, :], gateT[:, :, bass.ds(tile * S, P)], ALU.mult)\
                        .then_inc(s["yg_ready"], 1)
                if not last:
                    for par in range(2):
                        pool.wait_ge(s["y_done"], i * (2 * CH // 4) + (par + 1) * (CH // 4))
                        fill_chunk(par, i * 2 + (par + 2))

            pool.wait_ge(s["rem0"], NT)
            pool.wait_ge(s["sq_done"], NT)
            per_round = NT // (FIRST_TILE - 1)
            assert per_round * (FIRST_TILE - 1) == NT
            with pool.Fori(0, FIRST_TILE - 1) as i:
                for k in range(per_round):
                    n = i * per_round + k
                    nc.gpsimd.tensor_tensor(xc[:, n, :], xc[:, n, :], lnr[:, 2, :], ALU.mult)\
                        .then_inc(s["dx_ready"], 1)
                round_of(i, None, False)
            round_of(FIRST_TILE - 1, None, False)
            pool.wait_ge(s["dx_ready"], NT)
            round_of(FIRST_TILE, 0, False)
            with pool.Fori(FIRST_TILE + 1, ROUNDS - 1) as i:
                round_of(i, i - FIRST_TILE, False)
            round_of(ROUNDS - 1, IN_SCAN - 1, True)

        @block.scalar
        def _(act):
            act.wait_ge(s["rt_in"], 1)
            nc.scalar.activation(rt[:, 0:HALVES], var_e[:, 0:HALVES], ACT.Sqrt).then_inc(s["rt_out"], 1)
            act.wait_ge(s["ld_w"], 32)
            nc.scalar.activation(cond2[:, :, :], cond[:, :, :], ACT.Square)
            for ws in (slice(0, 2), slice(2, 5)):
                nc.scalar.activation(wsq[:, ws, :, :], w5[:, ws, :, :], ACT.Square).then_inc(s["wsq_ready"], 1)

            def take_xn(b, first):
                act.wait_ge(s["tr_done"], b + 1)
                if not first:
                    act.wait_ge(s["v_done"], b)
                nc.scalar.activation(xnT[:, :, :], bank[0][:, :].rearrange("p (k s) -> p k s", k=HT), ACT.Copy)\
                    .then_inc(s["xnT_ready"], 1)

            def take_qk(b, first):
                for w, name in enumerate("qk"):
                    act.wait_ge(s[f"{name}_done"], b + 1)
                    if not first:
                        act.wait_ge(s["part_ready"], b * 2)
                        act.wait_ge(s["pw"], b * (16 * NH // HT))
                    for o in range(HT):
                        ins = nc.scalar.activation(qk[:, w, o * S:(o + 1) * S], bank[1 + w][:, o * S:(o + 1) * S],
                                                   ACT.Copy, scale=dc[:, w, o, bass.ds(b, 1)])
                    ins.then_inc(s[f"{name}_in"], 1)
                    act.wait_ge(s[f"{name}_in"], b + 1)
                    nc.scalar.activation(part[:, w, 2 * w, :], qk[:, w, :], ACT.Copy).then_inc(s["cast0"], 1)
                for w in range(2):
                    act.wait_ge(s["rem_qk"], b * 2 + (w + 1))
                    nc.scalar.activation(part[:, w, 1, :], qk[:, w, :], ACT.Copy).then_inc(s["cast1"], 1)

            def take_vt(b):
                act.wait_ge(s["vt_done"], b + 1)
                for o in range(HT):
                    ins = nc.scalar.activation(vT[:, o, bass.ds(b * S, S)], bank[3][:, o * S:(o + 1) * S], ACT.Copy,
                                               scale=vdc[:, o, bass.ds(b, 1)])
                ins.then_inc(s["vt_in"], 1)

            def take_v(b, par, first):
                act.wait_ge(s["v_done"], b + 1)
                if not first:
                    act.wait_ge(s["pv_done"], b * 4 - 4)
                for t in range(HALVES):
                    src = bank[3][:, t * H:(t + 1) * H].rearrange("p (n r d) -> p n r d", r=2, d=HD)
                    ins = nc.scalar.activation(vp[:, par, t, :, 0:4:3, :], src, ACT.Copy)
                ins.then_inc(s["v_in"], 1)

            def sample(b, par, last):
                if not last:
                    take_xn(b + 1, False)
                    take_qk(b + 1, False)
                    take_vt(b + 1)
                act.wait_ge(s["mt_done"], b + 1)
                nc.scalar.activation(mT[:, :], bank[4][0:NH, 0:S], ACT.Copy).then_inc(s["mT_ready"], 1)
                act.wait_ge(s["mT_ready"], b + 1)
                act.dma_start(qst[96:97, par, :, :], mT[:, :]).then_inc(s["m_row"], 16)
                for n in range(NH):
                    g = n // 4
                    act.wait_ge(s["st_done"], b * NH + (n + 1))
                    if n % 4 == 0 and not (isinstance(b, int) and b == 0 and g < 2):
                        act.wait_ge(s["pv_done"], b * 4 + (g - 1))
                    nc.scalar.activation(ex[:, g % 2, n % 4, :], bank[4 + n % 4][:, :], ACT.Exp, scale=SCALE)\
                        .then_inc(s["exp_done"], 1)
                    if n == 3 and not last:
                        take_v(b + 1, 1 - par, isinstance(b, int) and b == 0)

            take_xn(0, True)
            act.wait_ge(s["rt_in"], 2)
            nc.scalar.activation(dct[:, 0:2, :, :], dcv[:, 0:2, :, :], ACT.Sqrt).then_inc(s["rt_out"], 1)
            act.wait_ge(s["dc_done"], 1)
            take_qk(0, True)
            act.wait_ge(s["rt_in"], 3)
            nc.scalar.activation(rt[:, HALVES:], var_e[:, HALVES:], ACT.Sqrt).then_inc(s["rt_out"], 1)
            act.wait_ge(s["rt_in"], 4)
            nc.scalar.activation(dct[:, 2:, :, :], dcv[:, 2:, :, :], ACT.Sqrt).then_inc(s["rt_out"], 1)
            act.wait_ge(s["dc_done"], 2)
            take_vt(0)
            act.wait_ge(s["const_pool"], 1)
            take_v(0, 0, True)
            sample(0, 0, False)
            with act.Fori(0, B // 2 - 1) as i:
                for k in range(2):
                    sample(i * 2 + (k + 1), (k + 1) % 2, False)
            sample(B - 1, 1, True)
            act.wait_ge(s["ld_l1"], 16 * 11)
            act.wait_ge(s["const_pool"], 2)
            act.wait_ge(s["x1_ready"], B)
            nc.scalar.activation(tA[:, :], tA[:, :], ACT.Tanh).then_inc(s["dt_out"], 1)

            def take_projection(b, first):
                act.wait_ge(s["xr_done"], b * 2 + 2)
                if not first:
                    act.wait_ge(s["conv_done"], b)
                for c in range(CT):
                    ins = nc.scalar.activation(xrp[:, c, TAPS - 1:], bank[4 + c // 2][:, (c % 2) * S:(c % 2 + 1) * S],
                                               ACT.Identity, bias=cond[:, c, bass.ds(b, 1)])
                ins.then_inc(s["xr_in"], 1)
                act.wait_ge(s["xr_in"], b + 1)
                for c in range(CT):
                    ins = nc.scalar.activation(acc[:, c, :], xrp[:, c, TAPS - 1:], ACT.Identity,
                                               bias=bcv[:, c:c + 1], scale=wcv[:, c, TAPS - 1:TAPS])
                ins.then_inc(s["tap3_ready"], 1)
                act.wait_ge(s["gate_done"], b * 2 + 2)
                for c2 in range(2):
                    ins = nc.scalar.activation(gateT[:, 2 * c2:2 * c2 + 2, bass.ds(b * S, S)],
                                               bank[6 + c2][:, :].rearrange("p (k s) -> p k s", k=2), ACT.Silu)
                ins.then_inc(s["gate_out"], 1)

            def take_tokens(b):
                for t in range(HALVES):
                    act.wait_ge(s["tok_ready"], b * HALVES + (t + 1))
                    nc.scalar.activation(xc[:, b * HALVES + t, :], bank[t][:, :], ACT.Copy)\
                        .then_inc(s["tok_taken"], 1)

            def gate_conv(b, first):
                act.wait_ge(s["conv_done"], b + 1)
                if not first:
                    act.wait_ge(s["xcT_used"], b)
                nc.scalar.activation(xcT[:, :, :], acc[:, :, :], ACT.Silu).then_inc(s["xcT_ready"], 1)

            take_projection(0, True)
            gate_conv(0, True)
            with act.Fori(1, B) as b:
                take_projection(b, False)
                take_tokens(b - 1)
                gate_conv(b, False)
            take_tokens(B - 1)
            act.wait_ge(s["rt_in"], 5)
            nc.scalar.activation(rt[:, :], var_e[:, :], ACT.Sqrt).then_inc(s["rt_out"], 1)
            def parts(b, k, first):
                for t in range(HALVES):
                    act.wait_ge(s["xn_ready"], b * HALVES + (t + 1))
                    if not first:
                        act.wait_ge(s[f"xs_out{k}"], 16 * HALVES)
                    nc.scalar.activation(xpart[:, HALVES * k + t, 0, :], xc[:, b * HALVES + t, :], ACT.Copy)\
                        .then_inc(s["part0"], 1)
                    if not (isinstance(b, int) and b == 0):
                        act.wait_ge(s["sq_done"], b * HALVES + (t - 1))
                    nc.scalar.activation(bank[6 + t][:, :], xc[:, b * HALVES + t, :], ACT.Square,
                                         accum_out=ss[:, bass.ds(b * HALVES + t, 1)]).then_inc(s["sq_done"], 1)
                for t in range(HALVES):
                    act.wait_ge(s["rem0"], b * HALVES + (t + 1))
                    nc.scalar.activation(xpart[:, HALVES * k + t, 1, :], xrem[:, t, :], ACT.Copy)\
                        .then_inc(s["part1"], 1)

            parts(0, 0, True)
            act.wait_ge(s["dt_in"], 1)
            nc.scalar.activation(dtt[:, :, :], dtt[:, :, :], ACT.Tanh).then_inc(s["dt_out"], 1)
            for b in range(1, B):
                parts(b, b % XS, b < XS)
            act.wait_ge(s["sq_done"], NT)
            nc.scalar.activation(nrm[:, :], ss[:, :], ACT.Sqrt).then_inc(s["nrm_ready"], 1)
            act.wait_ge(s["yb_done"], 1)
            nc.scalar.activation(ybias[:, :], bank[4][:, 0:S // 4], ACT.Copy).then_inc(s["ybias_ready"], 1)
            act.wait_ge(s["ybias_ready"], 1)

            def round_of(i, tile):
                for n in range(2 * CH // 4):
                    par, g = n // (CH // 4), n % (CH // 4)
                    if g == 0 and not (isinstance(i, int) and i == 0):
                        act.wait_ge(s[f"yst{par}"], i * 64)
                    act.wait_ge(s["y_done"], i * (2 * CH // 4) + (n + 1))
                    nc.scalar.activation(yb[:, par, g, :], bank[4 + n % 2][:, :], ACT.Identity,
                                         bias=ybias[:, bass.ds(i * (2 * CH // 4) + n, 1)]).then_inc(s["y_taken"], 1)
                    if tile is not None and n == 0:
                        first = isinstance(tile, int) and tile == 0
                        act.wait_ge(s["yt_done"], tile + 1)
                        if not first:
                            act.wait_ge(s["yg_ready"], tile)
                        nc.scalar.activation(yT[:, :, :], bank[6][:, :].rearrange("p (c s) -> p c s", c=CT), ACT.Copy)\
                            .then_inc(s["yt_taken"], 1)
                if tile is not None:
                    act.wait_ge(s["o_done"], tile + 1)
                    if not first:
                        act.wait_ge(s["o_out0"], tile * 16)
                    nc.scalar.activation(ob[:, 0, :], bank[7][:, 0:H], ACT.Copy).then_inc(s["ob_ready"], 1)
                    act.wait_ge(s["ob_ready"], tile + 1)
                    if isinstance(i, int) and i == ROUNDS - 1:
                        act.wait_ge(s["yst1"], ROUNDS * 64)
                    act.dma_start(out[tile, 0:P, :], ob[:, 0, :]).then_inc(s["o_out0"], 16)

            round_of(0, None)
            with act.Fori(1, FIRST_TILE) as i:
                round_of(i, None)
            round_of(FIRST_TILE, 0)
            with act.Fori(FIRST_TILE + 1, ROUNDS - 1) as i:
                round_of(i, i - FIRST_TILE)
            round_of(ROUNDS - 1, IN_SCAN - 1)
            stored = [IN_SCAN, 0]
            for n, (b, half) in enumerate(TAIL):
                t = n % 2
                act.wait_ge(s["to_done"], n + 1)
                if stored[t]:
                    act.wait_ge(s[f"o_out{t}"], stored[t] * 16)
                nc.scalar.activation(ob[:, t, :], bank[2 + t][:, 0:H], ACT.Copy).then_inc(s["tb_ready"], 1)
                act.wait_ge(s["tb_ready"], n + 1)
                act.dma_start(out[b, half * P:(half + 1) * P, :], ob[:, t, :]).then_inc(s[f"o_out{t}"], 16)
                stored[t] += 1
            for t in range(2):
                act.wait_ge(s[f"o_out{t}"], stored[t] * 16)

        @block.tensor
        def _(pe):
            mm = nc.tensor.matmul

            def style_sums(ws, bk):
                for w in ws:
                    for o in range(HT):
                        for k in range(HT):
                            st = cond2[:, (0 if w < 3 else HT) + k, :]
                            col = ((w - ws[0]) * HT + o) * B
                            ins = mm(bank[bk][:, col:col + B], wsq[:, w, k, o * P:(o + 1) * P], st, start=k == 0,
                                     stop=k == HT - 1)
                ins.then_inc(s["dcsum"], 1)

            def transpose_xn(b, first):
                pe.wait_ge(s["xnb_ready"], b + 1)
                if not first:
                    pe.wait_ge(s["att_ready"], b * 2 - 3)
                for k in range(HT):
                    for t in range(HALVES):
                        ins = nc.tensor.transpose(bank[0][:, k * S + t * P:k * S + (t + 1) * P],
                                                  xnb[:, t, k * P:(k + 1) * P], ident[:, :])
                ins.then_inc(s["tr_done"], 1)

            def channels_of(w, bk, done):
                for o in range(HT):
                    for k in range(HT):
                        ins = mm(bank[bk][:, o * S:(o + 1) * S], w5[:, w, k, o * P:(o + 1) * P],
                                 xnT[:, k, :], start=k == 0, stop=k == HT - 1)
                ins.then_inc(s[done], 1)

            def v_tokens(b):
                pe.wait_ge(s["vt_in"], b + 1)
                for t in range(HALVES):
                    for k in range(HT):
                        ins = mm(bank[3][:, t * H:(t + 1) * H], xnT[:, k, t * P:(t + 1) * P], w5[:, 2, k, :],
                                 start=k == 0, stop=k == HT - 1)
                ins.then_inc(s["v_done"], 1)

            def max_scores(b, par, n):
                if n >= 4:
                    pe.wait_ge(s["maxes"], b * NH + (n - 3))
                for t in range(HALVES):
                    ins = mm(bank[4 + n % 4][:, t * S:(t + 1) * S], qst[0:96, par, HEADS[n], t * P:(t + 1) * P],
                             kst[0:96, par, HEADS[n], :], start=True, stop=True)
                ins.then_inc(s["smax_done"], 1)

            def scores(b, par, g):
                for n in range(4 * g, 4 * g + 4):
                    if n >= 4:
                        pe.wait_ge(s["exp_done"], b * NH + (n - 3))
                    for t in range(HALVES):
                        ins = mm(bank[4 + n % 4][:, t * S:(t + 1) * S], kst[0:97, par, HEADS[n], t * P:(t + 1) * P],
                                 qst[0:97, par, HEADS[n], :], start=True, stop=True)
                    ins.then_inc(s["st_done"], 1)

            def weigh(b, buf, g, sums):
                o, par = g // 2, g % 2
                if sums:
                    pe.wait_ge(s["es_ready"], b * 4 + (g + 1))
                    for r in range(4):
                        ins = mm(bank[2 * o + 1][32 * r:32 * r + 32, 0:S], half_ones[:, par, :], esum[:, g % 2, r, :],
                                 start=par == 0, stop=par == 1, skip_group_check=True)
                    ins.then_inc(s["pv_done"], 1)
                    return
                pe.wait_ge(s["exp_done"], b * NH + (4 * g + 4))
                for t in range(HALVES):
                    for r in range(4):
                        mm(bank[2 * o][32 * r:32 * r + 32, 0:S],
                           vp[:, buf, t, 4 * o + r, 2 * par:2 * par + 2, :].rearrange("p a d -> p (a d)"),
                           ex[:, g % 2, r, t * S:(t + 1) * S], start=par == 0 and t == 0,
                           stop=par == 1 and t == HALVES - 1, skip_group_check=True)

            def project_att(b):
                pe.wait_ge(s["att_ready"], b * 2 + 2)
                for o in range(HT):
                    for k in range(HT):
                        mm(bank[0][:, o * S:(o + 1) * S], w5[:, 3, k, o * P:(o + 1) * P], attT[:, k, :],
                           start=k == 0, stop=k == HT - 1)

            def project_v(b):
                pe.wait_ge(s["vt_in"], b + 1)
                for o in range(HT):
                    for k in range(HT):
                        ins = mm(bank[1][:, o * S:(o + 1) * S], w5[:, 4, k, o * P:(o + 1) * P],
                                 vT[:, k, bass.ds(b * S, S)], start=k == 0, stop=k == HT - 1)
                ins.then_inc(s["wu_done"], 1)

            def weight_sums():
                for j, (lhs, rhs) in enumerate(((None, wxg), (lnb_rep, wx))):
                    for c in range(CT):
                        ins = mm(bank[0][:, 64 * j:64 * j + NP3], ones[:, :] if lhs is None else lhs[:, c, :],
                                 rhs[:, c, :], start=c == 0, stop=c == CT - 1)
                ins.then_inc(s["pconst"], 1)

            def early_maxima(b, par, turn):
                pe.wait_ge(s[f"ld_q{par}"], turn * 48 + 48)
                pe.wait_ge(s[f"ld_k{par}"], turn * 48 + 48)
                for n in range(EARLY):
                    max_scores(b, par, n)

            def sample(b, par, next_turn, first, last):
                def next_qkv(stage):
                    if last:
                        return
                    if stage == 0:
                        transpose_xn(b + 1, first)
                    elif stage == 1:
                        pe.wait_ge(s["xnT_ready"], b + 2)
                        if first:
                            pe.wait_ge(s["q_in"], b + 1)
                        channels_of(0, 1, "q_done")
                    elif stage == 2:
                        if first:
                            pe.wait_ge(s["k_in"], b + 1)
                        else:
                            pe.wait_ge(s["att_ready"], b * 2)
                        channels_of(1, 2, "k_done")
                    else:
                        if first:
                            pe.wait_ge(s["vt_in"], b + 1)
                        channels_of(2, 3, "vt_done")

                if first:
                    early_maxima(b, par, 0)
                for n in range(EARLY, NH):
                    if n == 4:
                        next_qkv(0)
                        next_qkv(1)
                    elif n in (7, 10):
                        next_qkv(2 if n == 7 else 3)
                    elif not first and n == 14:
                        project_att(b - 1)
                    max_scores(b, par, n)
                pe.wait_ge(s["maxes"], b * NH + NH)
                for t in range(HALVES):
                    ins = nc.tensor.transpose(bank[4][0:NH, t * P:(t + 1) * P], mx[:, t, :], ident[:, :])
                ins.then_inc(s["mt_done"], 1)
                if not last:
                    pe.wait_ge(s["q_in"], b + 2)
                if first:
                    weight_sums()
                else:
                    project_v(b - 1)
                pe.wait_ge(s["m_row"], b * 16 + 16)
                scores(b, par, 0)
                if not last:
                    v_tokens(b + 1)
                scores(b, par, 1)
                if first:
                    pe.wait_ge(s["wgain"], 2)
                else:
                    pe.wait_ge(s["x1_ready"], b)
                weigh(b, par, 0, False)
                scores(b, par, 2)
                weigh(b, par, 0, True)
                weigh(b, par, 1, False)
                scores(b, par, 3)
                weigh(b, par, 1, True)
                if not last:
                    pe.wait_ge(s["k_in"], b + 2)
                    pe.wait_ge(s["v_in"], b + 2)
                weigh(b, par, 2, False)
                weigh(b, par, 2, True)
                weigh(b, par, 3, False)
                if not last:
                    early_maxima(b + 1, 1 - par, next_turn)
                weigh(b, par, 3, True)

            def project_in(b, first, parts=(0, 1)):
                pe.wait_ge(s["x1_ready"], b + 1)
                for c in range(parts[0] * CT, (parts[-1] + 1) * CT):
                    if c == 0 and not first:
                        pe.wait_ge(s["xr_in"], b)
                    if c == CT and not first:
                        pe.wait_ge(s["gate_out"], b)
                    for k in range(HT):
                        ins = mm(bank[4 + c // 2][:, (c % 2) * S:(c % 2 + 1) * S], win[:, k, c * P:(c + 1) * P],
                                 xres[:, k, bass.ds(b * S, S)], start=k == 0, stop=k == HT - 1)
                    if c % 2:
                        ins.then_inc(s["xr_done"] if c < CT else s["gate_done"], 1)

            pe.wait_ge(s["ld_c"], 16 * 2)
            transpose_xn(0, True)
            pe.wait_ge(s["wsq_ready"], 1)
            style_sums((0, 1), 4)
            pe.wait_ge(s["xnT_ready"], 1)
            channels_of(0, 1, "q_done")
            channels_of(1, 2, "k_done")
            pe.wait_ge(s["wsq_ready"], 2)
            style_sums((2, 3, 4), 5)
            channels_of(2, 3, "vt_done")
            v_tokens(0)
            pe.wait_ge(s["ld_l1"], 16 * 11)
            for c in range(CT):
                ins = mm(bank[6][:, c * NS:(c + 1) * NS], wxd[:, c * P:(c + 1) * P], wdt[:, :], start=True, stop=True)
            ins.then_inc(s["wcomp"], 1)
            pe.wait_ge(s["const_pool"], 1)
            pe.wait_ge(s["wgain"], 1)
            pe.wait_ge(s["rt_in"], 4)
            sample(0, 0, 0, True, False)
            with pe.Fori(0, B // 2 - 1) as i:
                for k in range(2):
                    sample(i * 2 + (k + 1), (k + 1) % 2, i + 1, False, False)
            sample(B - 1, 1, None, False, True)
            pe.wait_ge(s["exp_done"], B * NH)
            project_in(0, True, (0,))
            project_att(B - 1)
            project_v(B - 1)
            project_in(0, True, (1,))

            def to_tokens(b, first):
                pe.wait_ge(s["xcT_ready"], b + 1)
                if not first:
                    pe.wait_ge(s["tok_taken"], b * HALVES)
                for t in range(HALVES):
                    for c in range(CT):
                        ins = nc.tensor.transpose(bank[t][:, c * P:(c + 1) * P], xcT[:, c, t * P:(t + 1) * P],
                                                  ident[:, :])
                    ins.then_inc(s["tok_ready"], 1)
                if not first:
                    pe.wait_ge(s["raw_ready"], b)
                for t in range(HALVES):
                    for c in range(CT):
                        ins = mm(bank[2][:, t * 64:t * 64 + NP3], xcT[:, c, t * P:(t + 1) * P], wxg[:, c, :],
                                 start=c == 0, stop=c == CT - 1)
                ins.then_inc(s["xcT_used"], 1)

            project_in(1, False)
            to_tokens(0, True)
            with pe.Fori(2, B) as b:
                project_in(b, False)
                to_tokens(b - 1, False)
            to_tokens(B - 1, False)
            pe.wait_ge(s["eb_ready"], 1)
            for j, src in enumerate((adt, cdt)):
                for t in range(HALVES):
                    ins = nc.tensor.transpose(bank[j][:, t * P:(t + 1) * P],
                                              src[:, t, :, :].rearrange("p b d -> p (b d)"), ident[:, :])
            ins.then_inc(s["eb_tr"], 1)
            pe.wait_ge(s["ipc_ready"], 1)
            for j, src in enumerate((ipc, dr)):
                for t in range(HALVES):
                    ins = nc.tensor.transpose(bank[2 + j][:, t * P:(t + 1) * P], src[:, t * P:(t + 1) * P],
                                              ident[:, :])
            ins.then_inc(s["eb_back"], 1)
            pe.wait_ge(s["ct_ready"], 1)
            for k in range(4):
                ins = mm(bank[4][32 * k:32 * k + 32, 0:S // 4], mask8[:, :],
                         ct10.rearrange("p (g k) -> p k g", k=4)[:, k, :], start=True, stop=True)
            ins.then_inc(s["yb_done"], 1)
            pe.wait_ge(s["bsplit"], 2)
            pe.wait_ge(s["c_ready"], 1)

            def u_steps(par, g, first, z_seen):
                for k in range(4):
                    step = 4 * g + k
                    if not first:
                        pe.wait_ge(s["z_ready"], z_seen + (step - 3))
                    mm(bank[k][:, :], bst[:, par, step, :], xst[:, par, step, :], start=True, stop=True)\
                        .then_inc(s["u_done"], 1)

            def y_steps(par, g, z_seen, y_seen):
                pe.wait_ge(s["z_ready"], z_seen + (4 * g + 4))
                if not (isinstance(y_seen, int) and y_seen <= 0):
                    pe.wait_ge(s["y_taken"], y_seen)
                for k in range(4):
                    step = 4 * g + k
                    ins = mm(bank[4 + g % 2][32 * k:32 * k + 32, :], cst[:, par, step, :], zst[:, step % ZR, :],
                             start=True, stop=True)
                ins.then_inc(s["y_done"], 1)

            G = CH // 4
            pe.wait_ge(s["ld_x0"], 16 * 3)
            pe.wait_ge(s["ld_b0"], 16)
            u_steps(0, 0, True, 0)

            def tile_transpose(tile, first):
                pe.wait_ge(s["ysum_ready"], tile + 1)
                if not first:
                    pe.wait_ge(s["yt_taken"], tile)
                for c in range(CT):
                    ins = nc.tensor.transpose(bank[6][:, c * P:(c + 1) * P], ysum[:, 0, c * P:(c + 1) * P],
                                              ident[:, :])
                ins.then_inc(s["yt_done"], 1)

            def tile_out(tile, first, part):
                if part == 0:
                    pe.wait_ge(s["yg_ready"], tile + 1)
                    if not first:
                        pe.wait_ge(s["ob_ready"], tile)
                for c in range(2 * part, 2 * part + 2):
                    mm(bank[7][:, 0:H], yg[:, 0, c, :], wo[:, c, :], start=c == 0, stop=False, skip_group_check=True)
                if part == 1:
                    pe.wait_ge(s["x1s_ready"], tile + 1)
                    for k in range(HT):
                        ins = mm(bank[7][:, k * P:(k + 1) * P], x1s[:, k, :], ident[:, :], start=False,
                                 stop=k == HT - 1, skip_group_check=True)
                    ins.then_inc(s["o_done"], 1)

            def round_of(i, tile, last):
                for n in range(2 * G):
                    par, g = n // G, n % G
                    nxt = (n + 1) % (2 * G)
                    if not (last and nxt == 0):
                        if nxt % G == 0:
                            q = nxt // G
                            load = i + (2 if q == 0 else 1)
                            pe.wait_ge(s[f"ld_x{q}"], load * (16 * 3))
                            pe.wait_ge(s[f"ld_b{q}"], load * 16)
                        u_steps(nxt // G, nxt % G, False, i * (2 * CH) + ((nxt // G) * CH if nxt else 2 * CH))
                    if g == 0:
                        pe.wait_ge(s["cst_ready"], i * 2 + (par + 1))
                    y_steps(par, g, i * (2 * CH) + par * CH, i * (2 * G) + (n - 1))
                    if tile is not None:
                        first = isinstance(tile, int) and tile == 0
                        if n == 0:
                            tile_transpose(tile, first)
                        elif n >= 2:
                            tile_out(tile, first, n - 2)

            pe.wait_ge(s["ybias_ready"], 1)
            round_of(0, None, False)
            with pe.Fori(1, FIRST_TILE) as i:
                round_of(i, None, False)
            round_of(FIRST_TILE, 0, False)
            with pe.Fori(FIRST_TILE + 1, ROUNDS - 1) as i:
                round_of(i, i - FIRST_TILE, False)
            round_of(ROUNDS - 1, IN_SCAN - 1, True)
            def tail_transpose(n):
                t = n % 2
                pe.wait_ge(s["tsum_ready"], n + 1)
                if n >= 2:
                    pe.wait_ge(s["tg_ready"], n - 1)
                for c in range(CT):
                    ins = nc.tensor.transpose(bank[t][:, c * P:(c + 1) * P], ysum[:, t, c * P:(c + 1) * P],
                                              ident[:, :])
                ins.then_inc(s["tt_done"], 1)

            tail_transpose(0)
            for n, (b, half) in enumerate(TAIL):
                t = n % 2
                if n == 1:
                    tail_transpose(1)
                if 1 <= n < len(TAIL) - 1:
                    tail_transpose(n + 1)
                pe.wait_ge(s["tg_ready"], n + 1)
                if n >= 2:
                    pe.wait_ge(s["tb_ready"], n - 1)
                for c in range(CT):
                    mm(bank[2 + t][:, 0:H], yg[:, t, c, :], wo[:, c, :], start=c == 0, stop=False,
                       skip_group_check=True)
                tok = b * S + half * P
                for k in range(HT):
                    ins = mm(bank[2 + t][:, k * P:(k + 1) * P], xres[:, k, tok:tok + P], ident[:, :], start=False,
                             stop=k == HT - 1, skip_group_check=True)
                ins.then_inc(s["to_done"], 1)

        @block.vector
        def _(dve):
            v = nc.vector
            own = Own(dve, s["vec_own"])

            def statistics(tiles, lo, hi):
                own.settle()
                for n in range(lo, hi):
                    own.mark(v.bn_stats(bn[:, n, :], tiles[:, n, :]))
                own.settle()
                for n in range(lo, hi):
                    own.mark(v.bn_aggr(mv[:, n, :], bn[:, n, :]))
                own.settle()
                v.tensor_scalar(var_e[:, lo:hi], mv[:, lo:hi, 1], EPS_LN, None, ALU.add).then_inc(s["rt_in"], 1)

            def rsqrt(y, root, x, tmp):
                own.mark(v.reciprocal(y, root))
                own.settle()
                own.mark(v.tensor_tensor(tmp, y, y, ALU.mult))
                own.settle()
                own.mark(v.tensor_tensor(tmp, tmp, x, ALU.mult))
                own.settle()
                own.mark(v.tensor_scalar(tmp, tmp, -0.5, 1.5, ALU.mult, ALU.add))
                own.settle()
                own.mark(v.tensor_tensor(y, y, tmp, ALU.mult))
                own.settle()

            def normalise(b, first):
                if not first:
                    dve.wait_ge(s["tr_done"], b)
                for t in range(HALVES):
                    n = b * HALVES + t
                    ins = v.tensor_scalar(xnb[:, t, :], xt[:, n, :], mv[:, n, 0:1], rs[:, bass.ds(n, 1)],
                                          ALU.subtract, ALU.mult)
                ins.then_inc(s["xnb_ready"], 1)

            def modulated_statistics(lo, hi):
                for n in range(lo, hi):
                    own.mark(v.tensor_tensor(xt[:, n, :], xt[:, n, :], s1b[:, n // HALVES, :], ALU.mult))
                statistics(xt, lo, hi)

            def demodulate(lo, hi, bk):
                v.tensor_scalar(dcv[:, lo:hi, :, :].rearrange("p w o b -> p (w o b)"),
                                bank[bk][:, 0:(hi - lo) * HT * B], EPS_DM, None, ALU.add).then_inc(s["rt_in"], 1)

            dve.wait_ge(s["ld_first"], 32)
            modulated_statistics(0, HALVES)
            dve.wait_ge(s["rt_in"], 1)
            dve.wait_ge(s["rt_out"], 1)
            rsqrt(rs[:, 0:HALVES], rt[:, 0:HALVES], var_e[:, 0:HALVES], rt[:, 0:HALVES])
            normalise(0, True)
            dve.wait_ge(s["dcsum"], 1)
            demodulate(0, 2, 4)
            dve.wait_ge(s["rt_in"], 2)
            dve.wait_ge(s["rt_out"], 2)
            rsqrt(dc[:, 0:2, :, :], dct[:, 0:2, :, :], dcv[:, 0:2, :, :], dct[:, 0:2, :, :])
            v.memset(tick[:, :], 0.0).then_inc(s["dc_done"], 1)
            dve.wait_ge(s["ld_rest"], 16)
            modulated_statistics(HALVES, NT)
            dve.wait_ge(s["rt_in"], 3)
            dve.wait_ge(s["rt_out"], 3)
            rsqrt(rs[:, HALVES:], rt[:, HALVES:], var_e[:, HALVES:], rt[:, HALVES:])
            normalise(1, False)
            dve.wait_ge(s["dcsum"], 2)
            demodulate(2, 5, 5)
            dve.wait_ge(s["rt_in"], 4)
            dve.wait_ge(s["rt_out"], 4)
            rsqrt(dc[:, 2:, :, :], dct[:, 2:, :, :], dcv[:, 2:, :, :], dct[:, 2:, :, :])
            own.mark(v.tensor_tensor(vdc[:, :, :], dc[:, 2, :, :], cond[:, HT:2 * HT, :], ALU.mult))
            own.settle()
            v.memset(tick[:, :], 0.0).then_inc(s["dc_done"], 1)
            dve.wait_ge(s["ld_x"], 16)
            dve.wait_ge(s["const_pool"], 1)

            def add_l0(b):
                dve.wait_ge(s["wu_done"], b + 1)
                for bk, w in ((0, 3), (1, 4)):
                    for o in range(HT):
                        tile = xres[:, o, bass.ds(b * S, S)]
                        ins = v.scalar_tensor_tensor(tile, bank[bk][:, o * S:(o + 1) * S], dc[:, w, o, bass.ds(b, 1)],
                                                     tile, ALU.mult, ALU.add)
                    if bk == 0:
                        own.mark(ins)
                        own.settle()
                ins.then_inc(s["x1_ready"], 1)

            def centre_projection():
                dve.wait_ge(s["pconst"], 1)
                own.mark(v.tensor_scalar(proj_mean[:, :], bank[0][:, 0:NP3], 1.0 / C, None, ALU.mult))
                own.mark(v.tensor_copy(proj_off[:, :], bank[0][:, 64:64 + NP3]))
                own.settle()
                own.mark(v.tensor_tensor(proj_off[:, 2 * NS:], proj_off[:, 2 * NS:], bdt[:, :], ALU.add))
                v.tensor_tensor(wxg[:, :, :], wxg[:, :, :], proj_mean[:, :].unsqueeze(1).broadcast_to([P, CT, NP3]),
                                ALU.subtract).then_inc(s["wgain"], 1)
                own.settle()

            def maxima(b, lo, hi):
                for n in range(lo, hi):
                    dve.wait_ge(s["smax_done"], b * NH + (n + 1))
                    v.tensor_reduce(mx[:, :, HEADS[n]:HEADS[n] + 1],
                                    bank[4 + n % 4][:, :].rearrange("p (t k) -> p t k", t=HALVES), AX.X, ALU.max)\
                        .then_inc(s["maxes"], 1)

            def sample(b, first, last, more):
                if first:
                    maxima(b, 0, EARLY)
                maxima(b, EARLY, NH)
                if first:
                    centre_projection()
                else:
                    add_l0(b - 1)

                def add_tiles(g):
                    dve.wait_ge(s["exp_done"], b * NH + (4 * g + 4))
                    if not (first and g < 2):
                        dve.wait_ge(s["pv_done"], b * 4 + (g - 1))
                    v.tensor_tensor(esum[:, g % 2, :, :], ex[:, g % 2, :, 0:S], ex[:, g % 2, :, S:], ALU.add)\
                        .then_inc(s["es_ready"], 1)

                def attend(o):
                    dve.wait_ge(s["pv_done"], b * 4 + (2 * o + 2))
                    own.mark(v.reciprocal(rec[:, o, :], bank[2 * o + 1][:, 0:S]))
                    own.settle()
                    v.scalar_tensor_tensor(attT[:, o, :], bank[2 * o][:, 0:S], vdc[:, o, bass.ds(b, 1)], rec[:, o, :],
                                           ALU.mult, ALU.mult).then_inc(s["att_ready"], 1)

                add_tiles(0)
                add_tiles(1)
                if more:
                    normalise(b + 2, False)
                add_tiles(2)
                attend(0)
                add_tiles(3)
                if not last:
                    dve.wait_ge(s["mt_done"], b + 1)
                    maxima(b + 1, 0, EARLY)
                attend(1)

            dve.wait_ge(s["ld_l1"], 16 * 11)
            dve.wait_ge(s["wcomp"], 1)
            own.mark(v.tensor_copy(wx[:, :, 2 * NS:], bank[6][:, 0:CT * NS].rearrange("p (c n) -> p c n", c=CT)))
            own.settle()
            for c in range(CT):
                v.tensor_scalar(wxg[:, c, :], wx[:, c, :], lnt[:, 0, c:c + 1], None, ALU.mult)
                ins = v.tensor_scalar(lnb_rep[:, c, :], ones[:, :], lnt[:, 1, c:c + 1], None, ALU.mult)
            ins.then_inc(s["wgain"], 1)
            sample(0, True, False, True)
            with dve.Fori(1, B - 2) as b:
                own.enter(b - 1, 3)
                sample(b, False, False, True)
            own.leave(B - 3)
            sample(B - 2, False, False, False)
            sample(B - 1, False, True, False)
            add_l0(B - 1)
            def convolve():
                for k in range(TAPS - 1):
                    for c in range(CT):
                        ins = v.scalar_tensor_tensor(acc[:, c, :], xrp[:, c, k:k + S], wcv[:, c, k:k + 1],
                                                     acc[:, c, :], ALU.mult, ALU.add)
                    if k < TAPS - 2:
                        own.mark(ins)
                        own.settle()
                ins.then_inc(s["conv_done"], 1)

            def take_raw(b):
                dve.wait_ge(s["tok_taken"], b * HALVES + HALVES)
                dve.wait_ge(s["xcT_used"], b + 1)
                v.tensor_copy(raw[:, bass.ds(b * HALVES, HALVES), :],
                              bank[2][:, 0:2 * 64].rearrange("p (t n) -> p t n", t=HALVES)[:, :, 0:NP3])\
                    .then_inc(s["raw_ready"], 1)
                for t in range(HALVES):
                    ins = v.bn_stats(bn[:, b * HALVES + t, :], xc[:, b * HALVES + t, :])
                own.mark(ins)

            dve.wait_ge(s["tap3_ready"], 1)
            convolve()
            with dve.Fori(1, B) as b:
                own.enter(b - 1, TAPS - 1)
                dve.wait_ge(s["tap3_ready"], b + 1)
                convolve()
                take_raw(b - 1)
            own.leave(B - 1)
            take_raw(B - 1)
            own.settle()
            for n in range(NT):
                own.mark(v.bn_aggr(mv[:, n, :], bn[:, n, :]))
            own.settle()
            v.tensor_scalar(var_e[:, :], mv[:, :, 1], EPS_LN, None, ALU.add).then_inc(s["rt_in"], 1)
            dve.wait_ge(s["rt_in"], 5)
            dve.wait_ge(s["rt_out"], 5)
            rsqrt(rs[:, :], rt[:, :], var_e[:, :], rt[:, :])
            def finish_rows(b):
                for t in range(HALVES):
                    n = b * HALVES + t
                    own.mark(v.scalar_tensor_tensor(xc[:, n, :], xc[:, n, :], mv[:, n, 0:1], lnr[:, 0, :],
                                                    ALU.subtract, ALU.mult))
                for t in range(HALVES):
                    own.settle(HALVES - 1 - t)
                    n = b * HALVES + t
                    v.scalar_tensor_tensor(xc[:, n, :], xc[:, n, :], rs[:, bass.ds(n, 1)], lnr[:, 1, :],
                                           ALU.mult, ALU.add).then_inc(s["xn_ready"], 1)

            def leave_first(b, k, first):
                for t in range(HALVES):
                    dve.wait_ge(s["part0"], b * HALVES + (t + 1))
                    if not first:
                        dve.wait_ge(s["parts_ready"], b * HALVES + (t - 1))
                    v.tensor_tensor(xrem[:, t, :], xc[:, b * HALVES + t, :], xpart[:, HALVES * k + t, 0, :],
                                    ALU.subtract).then_inc(s["rem0"], 1)

            def wide(ap):
                return ap.unsqueeze(2).broadcast_to([P, NT, NP3])

            def rows(ap):
                return ap.unsqueeze(1).broadcast_to([P, NT, ap.shape[1]])

            finish_rows(0)
            own.mark(v.tensor_tensor(raw[:, :, :], raw[:, :, :], wide(rs[:, :]), ALU.mult))
            own.settle()
            own.mark(v.tensor_tensor(raw[:, :, :], raw[:, :, :], rows(proj_off[:, :]), ALU.add))
            own.settle()
            v.tensor_copy(dtt[:, :, :], raw[:, :, 2 * NS:]).then_inc(s["dt_in"], 1)
            own.mark(v.tensor_copy(cdt[:, :, :, :].rearrange("p t b d -> p b t d"),
                                   raw[:, :, NS:2 * NS].rearrange("p (b t) d -> p b t d", t=HALVES)))
            finish_rows(1)
            leave_first(0, 0, True)
            dve.wait_ge(s["dt_out"], 2)
            own.mark(v.tensor_tensor(dtt[:, :, :], dtt[:, :, :], rows(tA[:, :]), ALU.mult))
            own.settle()
            v.tensor_scalar(adt[:, :, :, :].rearrange("p t b d -> p b t d"),
                            dtt[:, :, :].rearrange("p (b t) d -> p b t d", t=HALVES), -STEP, 1.0, ALU.mult, ALU.add)\
                .then_inc(s["eb_ready"], 1)
            finish_rows(2)
            leave_first(1, 1, False)
            dve.wait_ge(s["const_pool"], 3)
            dve.wait_ge(s["eb_tr"], 1)
            own.mark(v.tensor_tensor_scan(pcum[:, :], bank[0][:, 0:S], one_row[:, :], 1.0, ALU.mult, ALU.mult))
            own.settle()
            own.mark(v.reciprocal(ipc[:, :], pcum[:, :]))
            v.tensor_scalar(ct10, bank[1][:, 0:S], -BOUND, None, ALU.mult).then_inc(s["ct_ready"], 1)
            own.mark(v.tensor_tensor(cP[:, :], bank[1][:, 0:S], pcum[:, :], ALU.mult))
            own.settle()
            own.mark(v.tensor_scalar(rr[:, 1:], ipc[:, :], BOUND, None, ALU.mult))
            own.mark(v.tensor_scalar(hi[:, :], ipc[:, :], 2 * BOUND, None, ALU.mult))
            own.settle()
            v.tensor_tensor(dr[:, :], rr[:, 1:], rr[:, 0:S], ALU.subtract).then_inc(s["ipc_ready"], 1)
            v.memset(tick[:, :], 0.0).then_inc(s["c_ready"], 1)
            finish_rows(3)
            leave_first(2, 2, False)
            dve.wait_ge(s["eb_back"], 1)

            def split(parts, rem):
                flat = [parts[:, k, :, :].rearrange("p t n -> p (t n)") for k in range(3)]
                r = rem[:, :, :].rearrange("p t n -> p (t n)")
                for k in range(2):
                    own.mark(v.tensor_copy(flat[k], r))
                    own.settle()
                    own.mark(v.tensor_tensor(r, r, flat[k], ALU.subtract))
                    own.settle()
                v.tensor_copy(flat[2], r).then_inc(s["bsplit"], 1)

            own.mark(v.tensor_copy(rem[:, :, :].rearrange("p t n -> p (t n)"), bank[3][:, 0:S]))
            own.settle()
            split(dpart, rem)
            for b in range(XS, B):
                finish_rows(b)
                leave_first(b - 1, (b - 1) % XS, False)
            leave_first(B - 1, (B - 1) % XS, False)
            dve.wait_ge(s["nrm_ready"], 1)
            own.mark(v.tensor_scalar(nrm[:, :], nrm[:, :], 1.0, None, ALU.min))
            own.settle()
            own.mark(v.tensor_tensor(bnt[:, :, :, :].rearrange("p t b d -> p b t d"),
                                     raw[:, :, 0:NS].rearrange("p (b t) d -> p b t d", t=HALVES),
                                     nrm[:, :].rearrange("p (b t) -> p b t", t=HALVES).unsqueeze(3)
                                     .broadcast_to([P, B, HALVES, NS]), ALU.mult))
            own.settle()
            dve.wait_ge(s["bsplit"], 1)
            own.mark(v.tensor_tensor(rem[:, :, :].rearrange("p t n -> p (t n)"), bank[2][:, 0:S],
                                     bnt[:, :, :, :].rearrange("p t b d -> p (t b d)"), ALU.mult))
            own.settle()
            split(bpart, rem)
            for t in range(S):
                if t % 2 == 0:
                    dve.wait_ge(s["u_done"], t + 2)
                if t > 0:
                    dve.wait_ge(s["z_ready"], t)
                v._custom_dve(bass.dve_ops.TENSOR_ADD_SAT, out=zst[:, t % ZR, :], in0=zst[:, (t - 1) % ZR, :],
                              in1=bank[t % 4][:, :], s0=hi[:, t:t + 1], s1=0.0).then_inc(s["z_ready"], 1)
            def gate(n):
                b, half = TAIL[n]
                dve.wait_ge(s["tt_done"], n + 1)
                if n >= 2:
                    dve.wait_ge(s["to_done"], n - 1)
                tok = b * S + half * P
                v.tensor_tensor(yg[:, n % 2, :, :], bank[n % 2][:, :].rearrange("p (c s) -> p c s", c=CT),
                                gateT[:, :, tok:tok + P], ALU.mult).then_inc(s["tg_ready"], 1)

            dve.wait_ge(s["yt_done"], IN_SCAN)
            dve.wait_ge(s["o_done"], IN_SCAN)
            dve.wait_ge(s["dx_ready"], NT)
            for n, (b, half) in enumerate(TAIL):
                dve.wait_ge(s[f"ld_y{n % 4}"], 16 * (n // 4 + 1))
                if n >= 2:
                    dve.wait_ge(s["tt_done"], n - 1)
                v.tensor_tensor(ysum[:, n % 2, :], ytk[:, n % 4, :], xc[:, b * HALVES + half, :], ALU.add)\
                    .then_inc(s["tsum_ready"], 1)
                if n != 1:
                    gate(max(n - 1, 0))
            gate(len(TAIL) - 1)


def kernel(x, cond_2048, L0_cond_q_weight, L0_cond_k_weight, L0_cond_v_weight, L0_cond_w_weight, L0_cond_u_weight,
           L1_cond_W_in, L1_cond_W_conv, L1_cond_b_conv, L1_cond_ln_g, L1_cond_ln_b, L1_cond_W_xproj, L1_cond_W_dt,
           L1_cond_b_dt, L1_cond_A_log, L1_cond_D, L1_cond_W_out):
    import concourse.bacc as bacc
    from concourse.bass_utils import run_bass_kernel_spmd

    def channels(a, width):
        return np.asarray(a).reshape(-1, P, width).transpose(1, 0, 2)

    x, cond = np.asarray(x), np.asarray(cond_2048)
    w5 = np.stack([channels(np.asarray(w).T, H) for w in (L0_cond_q_weight, L0_cond_k_weight, L0_cond_v_weight,
                                                          L0_cond_w_weight, L0_cond_u_weight)], axis=1)
    per_channel = [np.asarray(a).reshape(CT, P).T for a in (L1_cond_ln_g, L1_cond_ln_b)]
    p = np.arange(P)
    arrays = {
        "x_tok": x.reshape(NT, P, H).transpose(1, 0, 2),
        "xT": channels(x.reshape(B * S, H).T, B * S),
        "s1_row": cond[:, :H],
        "condT": channels(cond.T, B),
        "w5T": w5,
        "winT": channels(np.asarray(L1_cond_W_in).T, 2 * C),
        "wconv": np.asarray(L1_cond_W_conv).reshape(CT, P, TAPS).transpose(1, 0, 2),
        "bconv": np.asarray(L1_cond_b_conv).reshape(CT, P).T,
        "ln_row": np.stack([np.asarray(a) for a in (L1_cond_ln_g, L1_cond_ln_b, L1_cond_D)]),
        "lnT": np.stack(per_channel, axis=1),
        "wxT": channels(np.asarray(L1_cond_W_xproj).T, NP3),
        "wxdt": np.asarray(L1_cond_W_xproj)[2 * NS:],
        "wdtT": np.asarray(L1_cond_W_dt).T,
        "bdt_row": np.asarray(L1_cond_b_dt),
        "alog_row": np.asarray(L1_cond_A_log),
        "woT": channels(np.asarray(L1_cond_W_out).T, H),
        "ident_d": np.eye(P, dtype=np.float32),
        "mask8_d": (p[:, None] // NS == np.arange(32)).astype(np.float32),
    }
    arrays = {k: np.ascontiguousarray(a) for k, a in arrays.items()}
    nc = bacc.Bacc("TRN2", target_bir_lowering=False, num_devices=1)
    aps = {k: nc.dram_tensor(k, a.shape, mybir.dt.from_np(a.dtype), kind="ExternalInput").ap()
           for k, a in arrays.items()}
    out = nc.dram_tensor("out", (B, S, H), F32, kind="ExternalOutput").ap()
    build(nc, *aps.values(), out)
    r = run_bass_kernel_spmd(nc, [arrays], core_ids=[0])
    return r.results[0]["out"]
```
